# Optimizing a Trainium2 kernel written in Bass

```python
import numpy as np
import jax
import jax.numpy as jnp

def _softmax(x, axis=-1):
    return jax.nn.softmax(x, axis=axis)

def _gelu(x):
    return jax.nn.gelu(x, approximate=True)

def _silu(x):
    return jax.nn.silu(x)

def _sigmoid(x):
    return jax.nn.sigmoid(x)

def _layernorm(x, axis=-1, eps=1e-05):
    m = jnp.mean(x, axis=axis, keepdims=True)
    v = jnp.var(x, axis=axis, keepdims=True)
    return (x - m) / jnp.sqrt(v + eps)

def _scatter_add(tgt, idx, src, axis=0):
    return tgt.at[idx].add(src)

def _segment_sum(src, seg, n):
    return jax.ops.segment_sum(src, seg, n)
kernel_name = 'mk_decoder_postln_d1_seqx_r8_e45917'

def setup_inputs(seed: int=0):
    np.random.seed(seed)
    _w = jnp.asarray

    def _rec_inputs():
        import jax
        import jax.numpy as jnp
        _rk = jax.random.key(seed)
        x = 7.22e-05 + 1 * jax.random.normal(jax.random.fold_in(_rk, 1), (4, 256, 128), jnp.float32)
        _lenS = 256 - jax.random.randint(jax.random.fold_in(_rk, 7), (4,), 0, max(1, 256 // 4) + 1, jnp.int32)
        _lenS2 = 512 - jax.random.randint(jax.random.fold_in(_rk, 8), (4,), 0, max(1, 512 // 4) + 1, jnp.int32)
        _ctx_1024P = jax.random.normal(jax.random.fold_in(_rk, 11), (4, 16, 128), jnp.float32)
        _ctx_1024c = jax.random.dirichlet(jax.random.fold_in(_rk, 511), 0.3 * jnp.ones((16,), jnp.float32), (4, 512))
        _ctx_1024t = jnp.einsum('bsk,bkd->bsd', _ctx_1024c, _ctx_1024P)
        _ctx_1024t = _ctx_1024t * jax.lax.rsqrt(jnp.mean(jnp.square(_ctx_1024t)) + 1e-12) * 0.953939
        ctx_1024 = 4.13588e-05 + 0.999923 * (_ctx_1024t + 0.3 * jax.random.normal(jax.random.fold_in(_rk, 611), (4, 512, 128), jnp.float32))
        return (x, ctx_1024)
    x, ctx_1024 = _rec_inputs()

    def _L0_attn_setup():
        import jax, jax.numpy as jnp
        import numpy as np
        import math
        D_MODEL = 128
        N_HEADS = 16
        DECAY_SCALE = 0.25

        def power_law_mask(n, decay_scale):
            i = jnp.arange(n)[:, None]
            j = jnp.arange(n)[None, :]
            delta = (i - j).astype(jnp.float32)
            decay = jnp.where(delta > 0, -decay_scale * jnp.log(jnp.maximum(delta, 1.0)), 0.0)
            return jnp.where(j > i, -jnp.inf, decay)
        key = jax.random.key(seed)
        ks = jax.random.split(key, 9)
        B, N, D = (2, 256, D_MODEL)
        s = 1.0 / math.sqrt(D)
        return {'x': jax.random.normal(ks[0], (B, N, D), dtype=jnp.float32), 'Wq': jax.random.normal(ks[1], (D, D), dtype=jnp.float32) * s, 'bq': jnp.zeros((D,), dtype=jnp.float32), 'Wk': jax.random.normal(ks[2], (D, D), dtype=jnp.float32) * s, 'bk': jnp.zeros((D,), dtype=jnp.float32), 'Wv': jax.random.normal(ks[3], (D, D), dtype=jnp.float32) * s, 'bv': jnp.zeros((D,), dtype=jnp.float32), 'Wo': jax.random.normal(ks[4], (D, D), dtype=jnp.float32) * s, 'bo': jnp.zeros((D,), dtype=jnp.float32)}
    _L0_attn_all = _L0_attn_setup()
    _L0_attn_in = {k: v for k, v in _L0_attn_all.items() if k in ('Wq', 'bq', 'Wk', 'bk', 'Wv', 'bv', 'Wo', 'bo')}
    del _L0_attn_all

    def _L0_xattn_setup():
        import jax, jax.numpy as jnp
        import numpy as np
        D = 128
        B, S = (4, 256)
        key = jax.random.key(seed)
        ks = jax.random.split(key, 9)
        scale = 1.0 / np.sqrt(D)
        return {'queries': jax.random.normal(ks[0], (B, S, D), dtype=jnp.float32), 'keys': jax.random.normal(ks[1], (B, S, D), dtype=jnp.float32), 'values': jax.random.normal(ks[2], (B, S, D), dtype=jnp.float32), 'Wq': jax.random.uniform(ks[3], (D, D), jnp.float32, -scale, scale), 'bq': jax.random.uniform(ks[4], (D,), jnp.float32, -scale, scale), 'Wk': jax.random.uniform(ks[5], (D, D), jnp.float32, -scale, scale), 'bk': jax.random.uniform(ks[6], (D,), jnp.float32, -scale, scale), 'Wv': jax.random.uniform(ks[7], (D, D), jnp.float32, -scale, scale), 'bv': jax.random.uniform(ks[8], (D,), jnp.float32, -scale, scale)}
    _L0_xattn_all = _L0_xattn_setup()
    _L0_xattn_in = {k: v for k, v in _L0_xattn_all.items() if k in ('Wq', 'bq', 'Wk', 'bk', 'Wv', 'bv')}
    del _L0_xattn_all

    def _L0_ffn_setup():
        import jax, jax.numpy as jnp
        import numpy as np
        D_MODEL, D_FF, N_EXP = (128, 512, 8)
        key = jax.random.key(seed)
        ks = jax.random.split(key, 8)
        s = lambda fan_in: 1.0 / np.sqrt(fan_in)
        x = jax.random.normal(ks[0], (4, 256, D_MODEL), dtype=jnp.float32)
        Wr = jax.random.uniform(ks[1], (N_EXP, D_MODEL), jnp.float32, -s(D_MODEL), s(D_MODEL))
        br = jax.random.uniform(ks[2], (N_EXP,), jnp.float32, -s(D_MODEL), s(D_MODEL))
        W1 = jax.random.uniform(ks[3], (N_EXP, D_FF, D_MODEL), jnp.float32, -s(D_MODEL), s(D_MODEL))
        b1 = jax.random.uniform(ks[4], (N_EXP, D_FF), jnp.float32, -s(D_MODEL), s(D_MODEL))
        W2 = jax.random.uniform(ks[5], (N_EXP, D_MODEL, D_FF), jnp.float32, -s(D_FF), s(D_FF))
        b2 = jax.random.uniform(ks[6], (N_EXP, D_MODEL), jnp.float32, -s(D_FF), s(D_FF))
        return {'x': x, 'Wr': Wr, 'br': br, 'W1': W1, 'b1': b1, 'W2': W2, 'b2': b2}
    _L0_ffn_all = _L0_ffn_setup()
    _L0_ffn_in = {k: v for k, v in _L0_ffn_all.items() if k in ('Wr', 'br', 'W1', 'b1', 'W2', 'b2')}
    del _L0_ffn_all
    return {'x': x, 'ctx_1024': ctx_1024, 'L0_attn_Wq': _L0_attn_in['Wq'], 'L0_attn_bq': _L0_attn_in['bq'], 'L0_attn_Wk': _L0_attn_in['Wk'], 'L0_attn_bk': _L0_attn_in['bk'], 'L0_attn_Wv': _L0_attn_in['Wv'], 'L0_attn_bv': _L0_attn_in['bv'], 'L0_attn_Wo': _L0_attn_in['Wo'], 'L0_attn_bo': _L0_attn_in['bo'], 'L0_xattn_Wq': _L0_xattn_in['Wq'], 'L0_xattn_bq': _L0_xattn_in['bq'], 'L0_xattn_Wk': _L0_xattn_in['Wk'], 'L0_xattn_bk': _L0_xattn_in['bk'], 'L0_xattn_Wv': _L0_xattn_in['Wv'], 'L0_xattn_bv': _L0_xattn_in['bv'], 'L0_ffn_Wr': _L0_ffn_in['Wr'], 'L0_ffn_br': _L0_ffn_in['br'], 'L0_ffn_W1': _L0_ffn_in['W1'], 'L0_ffn_b1': _L0_ffn_in['b1'], 'L0_ffn_W2': _L0_ffn_in['W2'], 'L0_ffn_b2': _L0_ffn_in['b2']}

def reference(x, ctx_1024, L0_attn_Wq, L0_attn_bq, L0_attn_Wk, L0_attn_bk, L0_attn_Wv, L0_attn_bv, L0_attn_Wo, L0_attn_bo, L0_xattn_Wq, L0_xattn_bq, L0_xattn_Wk, L0_xattn_bk, L0_xattn_Wv, L0_xattn_bv, L0_ffn_Wr, L0_ffn_br, L0_ffn_W1, L0_ffn_b1, L0_ffn_W2, L0_ffn_b2):
    import jax
    import jax.numpy as jnp

    def _L0_attn_ref(x, Wq, bq, Wk, bk, Wv, bv, Wo, bo):
        import jax, jax.numpy as jnp
        import numpy as np
        import math
        D_MODEL = 128
        N_HEADS = 16
        DECAY_SCALE = 0.25

        def power_law_mask(n, decay_scale):
            i = jnp.arange(n)[:, None]
            j = jnp.arange(n)[None, :]
            delta = (i - j).astype(jnp.float32)
            decay = jnp.where(delta > 0, -decay_scale * jnp.log(jnp.maximum(delta, 1.0)), 0.0)
            return jnp.where(j > i, -jnp.inf, decay)
        B, N, D = x.shape
        H = N_HEADS
        dk = D // H

        def proj(W, b):
            return (x @ W + b).reshape(B, N, H, dk).transpose(0, 2, 1, 3)
        Q, K, V = (proj(Wq, bq), proj(Wk, bk), proj(Wv, bv))
        scores = jnp.einsum('bhnd,bhmd->bhnm', Q, K) / jnp.sqrt(jnp.float32(dk))
        scores = scores + power_law_mask(N, DECAY_SCALE)[None, None]
        attn = jax.nn.softmax(scores, axis=-1)
        out = jnp.einsum('bhnm,bhmd->bhnd', attn, V)
        out = out.transpose(0, 2, 1, 3).reshape(B, N, D)
        return out @ Wo + bo

    def _L0_xattn_ref(queries, keys, values, Wq, bq, Wk, bk, Wv, bv):
        import jax, jax.numpy as jnp
        import numpy as np
        D = 128
        B, S = (4, 256)
        Q = jnp.einsum('bsd,ed->bse', queries, Wq) + bq
        K = jnp.einsum('bsd,ed->bse', keys, Wk) + bk
        V = jnp.einsum('bsd,ed->bse', values, Wv) + bv
        scores = jax.nn.relu(jnp.einsum('bqd,bkd->bqk', Q, K))
        return jnp.einsum('bqk,bkd->bqd', scores, V)

    def _L0_ffn_ref(x, Wr, br, W1, b1, W2, b2):
        import jax, jax.numpy as jnp
        import numpy as np
        D_MODEL, D_FF, N_EXP = (128, 512, 8)
        B, S, D = x.shape
        xf = x.reshape(-1, D)
        logits = xf @ Wr.T + br
        expert_idx = jnp.argmax(logits, axis=-1)
        h = jax.nn.relu(jnp.einsum('td,efd->etf', xf, W1) + b1[:, None, :])
        y = jnp.einsum('etf,edf->etd', h, W2) + b2[:, None, :]
        out = y[expert_idx, jnp.arange(xf.shape[0])]
        return out.reshape(B, S, D)
    x = _layernorm(x + _L0_attn_ref(x, L0_attn_Wq, L0_attn_bq, L0_attn_Wk, L0_attn_bk, L0_attn_Wv, L0_attn_bv, L0_attn_Wo, L0_attn_bo), axis=-1)
    x = _layernorm(x + _L0_xattn_ref(x, ctx_1024, ctx_1024, L0_xattn_Wq, L0_xattn_bq, L0_xattn_Wk, L0_xattn_bk, L0_xattn_Wv, L0_xattn_bv), axis=-1)
    x = _layernorm(x + _L0_ffn_ref(x, L0_ffn_Wr, L0_ffn_br, L0_ffn_W1, L0_ffn_b1, L0_ffn_W2, L0_ffn_b2), axis=-1)
    return x

_drawn_inputs = setup_inputs


def setup_inputs(seed=0):
    import zlib

    import numpy as np

    out = dict(_drawn_inputs(seed))
    spreads = {'L0_attn_bq': (0.0, 0.329),
     'L0_attn_bk': (0.0, 0.8),
     'L0_attn_bv': (0.0, 0.1),
     'L0_attn_bo': (0.0, 0.1)}
    factors = {'L0_ffn_b1': 2.924}
    for name, (base, spread) in spreads.items():
        noise = np.random.default_rng([zlib.crc32(name.encode()), seed]).standard_normal(out[name].shape)
        drawn = base * np.exp(spread * noise) if base else spread * noise
        out[name] = jnp.asarray(drawn.astype(out[name].dtype))
    for name, factor in factors.items():
        out[name] = (out[name] * factor).astype(out[name].dtype)
    return out
```

```python
from contextlib import ExitStack

import concourse.bass as bass
from concourse import mybir

F32 = mybir.dt.float32
BF16 = mybir.dt.bfloat16
I32 = mybir.dt.int32
U32 = mybir.dt.uint32
ALU = mybir.AluOpType
ACT = mybir.ActivationFunctionType
AX = mybir.AxisListType

P = 128
B, S, D = 4, 256, 128
NT = S // P
TILES = B * NT
H = 16
DK = D // H
SK = 512
KT = SK // P
E, FF = 8, 512
FC = FF // P
PARTS = 3
TERM = PARTS * PARTS * DK
MROW = 96
VW = 32
EPS = 1e-5
DECAY = 0.25
SHUT = -1e30
CEIL = 1e30

UNITS = [(0, 0, 4), (0, 4, 4), (1, 0, 8), (0, 8, 4), (0, 12, 4), (1, 8, 8)]
NU = len(UNITS)
KBUF = 3
EBUF = 7


def schedule():
    out = [("proj", 0, 0), ("proj", 1, 0), ("ctx", 0, 0), ("ctx", 1, 0)]
    out += [("max", 0, u) for u in range(NU)] + [("shift", 0, 0)]
    for b in range(B + 1):
        c = b - 1
        row = [("exp", b, 0), ("pv", c, 2), ("max", b + 1, 0), ("pv", c, 3), ("evac", c, 0), ("proj", b + 2, 0),
               ("exp", b, 1), ("turn", c, 0), ("max", b + 1, 1), ("back", c, 0),
               ("exp", b, 2), ("out", c, 0), ("max", b + 1, 2),
               ("exp", b, 3), ("x1t", c, 0), ("max", b + 1, 3), ("q2", c, 0),
               ("exp", b, 4), ("pv", b, 0), ("max", b + 1, 4), ("relu", c, 0),
               ("exp", b, 5), ("pv", b, 1), ("max", b + 1, 5), ("shift", b + 1, 0),
               ("cross", c, 0), ("ctx", b + 2, 0), ("x2t", c, 0), ("route", c, 0)]
        out += [p for p in row if 0 <= p[1] < B]
    return out


USES = {"proj": "mm", "ctx": "mm", "max": "s", "shift": "m", "exp": "s", "back": "m", "out": "m",
        "x1t": "m", "q2": "m", "relu": "s", "cross": "m", "x2t": "m", "route": "m"}


def slots(order):
    at = {"s": 0, "m": 0}
    out = {}
    for piece in order:
        for j, ring in enumerate(USES.get(piece[0], "")):
            out[(*piece, j)] = (at[ring] % 2, at[ring] // 2)
            at[ring] += 1
    return out, at


def decoder_kernel(nc, xtok, xT, ctxT, wts, cols, rows, w1T, w2T, b1c, b2r, out):
    order = schedule()
    place, used = slots(order)
    WQ, WK, WV, WO, XQ, XK, XV, WR = range(8)
    BQ, BK, XBQ, XBK = range(4)
    BV, BO, XBV, BR = range(4)

    parts_dram = nc.dram_tensor("parts_dram", [B, PARTS, 2, D, S], BF16, kind="Internal").ap()

    with ExitStack() as ctx:
        def sb(name, shape, dt=F32):
            return ctx.enter_context(nc.sbuf_tensor(name, shape, dt))

        def psum(name, cols_):
            return ctx.enter_context(nc.psum_tensor(name, [P, cols_], F32))

        def sem(name):
            return ctx.enter_context(nc.semaphore(name))

        w_sb = sb("w_sb", [P, 7 * D + E])
        cols_sb = sb("cols_sb", [P, 4])
        rows_sb = sb("rows_sb", [P, 3 * D + E])
        xT_sb = sb("xT_sb", [P, B * S])
        x_sb = sb("x_sb", [P, TILES, D])
        ctxT_sb = sb("ctxT_sb", [P, B * SK])
        w1_sb = sb("w1_sb", [P, E, FF])
        w2_sb = sb("w2_sb", [P, E, FC, D])
        b1_sb = sb("b1_sb", [P, E * FC])
        b2_sb = sb("b2_sb", [1, E, D])

        def W(i):
            return w_sb[:, i * D:(i + 1) * D] if i < WR else w_sb[:, WR * D:WR * D + E]

        def R(i):
            return rows_sb[:, i * D:(i + 1) * D] if i < BR else rows_sb[:, BR * D:BR * D + E]

        ident = sb("ident", [P, P])
        identb = sb("identb", [P, P], BF16)
        ones_row = sb("ones_row", [1, P])
        maskb = sb("maskb", [P, 4, P], BF16)
        delta = sb("delta", [P, S], I32)
        deltaf = sb("deltaf", [P, S])
        decay = sb("decay", [P, S])
        mhalf = sb("mhalf", [P, 16])
        rank8 = sb("rank8", [P, E])
        rank8i = sb("rank8i", [P, E], I32)
        bqs = sb("bqs", [P, 1])

        qk32 = sb("qk32", [P, 2, 2 * S])
        rest = sb("rest", [P, 2, 2 * S])
        parts = sb("parts", [P, 2, PARTS, 2 * S], BF16)
        qx = sb("qx", [P, KBUF, H, S], BF16)
        kx = sb("kx", [P, KBUF, H, S], BF16)
        vx = sb("vx", [P, KBUF, NT, H, VW])
        mx = sb("mx", [P, 2, H, NT])
        mshift = sb("mshift", [2 * H, 2, 2, P], BF16)
        es = sb("es", [P, EBUF, 1024])
        osb = sb("osb", [P, 4, S])
        rden = sb("rden", [P, NT, H])
        attn = sb("attn", [P, NT, D])
        attnT = sb("attnT", [P, S])
        xb = x_sb
        z = sb("z", [P, NT, D])
        stats = sb("stats", [P, NT, 6])
        mv = sb("mv", [P, NT, 2])
        rstd = sb("rstd", [P, NT])
        var = sb("var", [P, NT])
        stats4 = sb("stats4", [P, 4, 6])
        mv4 = sb("mv4", [P, 4, 2])
        var4 = sb("var4", [P, 4])
        rstd4 = sb("rstd4", [P, 4])
        x1 = sb("x1", [P, TILES, D])
        x1T = sb("x1T", [P, S])
        q2T = sb("q2T", [P, S])
        k2T = sb("k2T", [P, KBUF, SK])
        v2 = sb("v2", [P, KBUF, KT, D])
        sc2 = sb("sc2", [P, KT, S])
        x2 = sb("x2", [P, TILES, D])
        x2T = sb("x2T", [P, B * S])
        lg = sb("lg", [P, NT, E])
        lgmax = sb("lgmax", [P, NT])
        hot = sb("hot", [P, TILES, E])
        hT = es[:, 0:4, :].rearrange("p (i a) (b n) -> p i (a b) n", i=2, b=2)
        acc = x1
        yout = x_sb

        ps_s = [psum(f"ps_s{i}", 1024) for i in range(2)]
        ps_m = [psum(f"ps_m{i}", 512) for i in range(2)]
        ps_o = psum("ps_o", 1024)

        s_full = [sem(f"s_full{i}") for i in range(2)]
        s_free = [sem(f"s_free{i}") for i in range(2)]
        m_full = [sem(f"m_full{i}") for i in range(2)]
        m_free = [sem(f"m_free{i}") for i in range(2)]
        ring = {"s": (ps_s, s_full, s_free), "m": (ps_m, m_full, m_free)}

        ld_w = sem("ld_w")
        ld_rows = sem("ld_rows")
        ld_x0 = sem("ld_x0")
        ld_xT = sem("ld_xT")
        ld_x = sem("ld_x")
        ld_ctx = sem("ld_ctx")
        ld_ffn = sem("ld_ffn")
        stored = [sem(f"stored{b}") for b in range(B)]
        spread = [sem(f"spread{b}") for b in range(B)]
        shifted = [sem(f"shifted{b}") for b in range(B)]
        pool_done = sem("pool_done")
        consts = sem("consts")
        zeroed = sem("zeroed")
        xb_ready = sem("xb_ready")
        decay_ready = sem("decay_ready")
        dve = sem("dve")
        var_ready = sem("var_ready")
        rstd_ready = sem("rstd_ready")
        qk_ready = sem("qk_ready")
        parts_ready = sem("parts_ready")
        mhi_ready = sem("mhi_ready")
        exp_ready = sem("exp_ready")
        p_ready = sem("p_ready")
        pv_done = sem("pv_done")
        osb_ready = sem("osb_ready")
        turned = sem("turned")
        attn_ready = sem("attn_ready")
        x1_ready = sem("x1_ready")
        x2_ready = sem("x2_ready")
        hot_ready = sem("hot_ready")
        y_out = sem("y_out")
        done = sem("done")

        block = ctx.enter_context(nc.Block())

        def filled(eng, name, piece, j=0):
            slot, n = place[(*piece, j)]
            eng.wait_ge(ring[name][1][slot], n + 1)
            return ring[name][0][slot], ring[name][2][slot]

        def taken(eng, name, piece, j=0):
            slot, n = place[(*piece, j)]
            eng.wait_ge(ring[name][2][slot], n + 1)

        def vacant(pe, name, piece, j=0):
            slot, n = place[(*piece, j)]
            if n:
                pe.wait_ge(ring[name][2][slot], n)
            return ring[name][0][slot], ring[name][1][slot]

        @block.sync
        def _(sp):
            sp.dma_start(w_sb[:, 0:3 * D], wts[:, 0:3 * D]).then_inc(ld_x0, 16)
            sp.dma_start(xT_sb[:, 0:S], xT[:, 0:S]).then_inc(ld_x0, 16)
            sp.dma_start(cols_sb[:, :], cols).then_inc(ld_x0, 16)
            sp.dma_start(xT_sb[:, S:], xT[:, S:]).then_inc(ld_xT, 16)
            sp.dma_start(w_sb[:, 3 * D:], wts[:, 3 * D:]).then_inc(ld_w, 16)
            sp.dma_start(ctxT_sb[:, :], ctxT).then_inc(ld_ctx, 16)
            sp.dma_start(x_sb[:, :, :], xtok.rearrange("(n p) d -> p n d", p=P)).then_inc(ld_x, 16)
            for kind, b, _i in order:
                if kind == "proj":
                    sp.wait_ge(parts_ready, b + 1)
                    sp.dma_start(parts_dram[b].rearrange("i w p t -> p i w t"),
                                 parts[:, b % 2, :, :].rearrange("p i (w t) -> p i w t", w=2)).then_inc(stored[b], 16)
                    sp.wait_ge(stored[b], 16)
                    sp.wait_ge(zeroed, min(2 * b + 2, B + KBUF))
                    if b >= KBUF:
                        filled(sp, "s", ("exp", b - KBUF, NU - 1))
                    for i in range(PARTS):
                        for j in range(PARTS):
                            at = (PARTS * i + j) * DK
                            sp.dma_start(qx[at:at + DK, b % KBUF, :, :],
                                         parts_dram[b, i, 0].rearrange("(h d) t -> d h t", d=DK)).then_inc(spread[b], 16)
                            sp.dma_start(kx[at:at + DK, b % KBUF, :, :],
                                         parts_dram[b, j, 1].rearrange("(h d) t -> d h t", d=DK)).then_inc(spread[b], 16)
                    if b == 1:
                        sp.dma_start(w1_sb[:, :, :], w1T.rearrange("p (e f) -> p e f", e=E)).then_inc(ld_ffn, 16)
                        sp.dma_start(w2_sb[:, :, :, :],
                                     w2T.rearrange("p (e c d) -> p e c d", e=E, c=FC)).then_inc(ld_ffn, 16)
                        sp.dma_start(b1_sb[:, :], b1c).then_inc(ld_ffn, 16)
                        sp.dma_start(b2_sb[:, :, :], b2r.rearrange("(a e) d -> a e d", a=1)).then_inc(ld_ffn, 16)
                if kind == "shift":
                    taken(sp, "m", ("shift", b, 0))
                    for i in range(2):
                        sp.dma_start(qx[MROW + i:MROW + i + 1, b % KBUF, :, :].rearrange("o h (t q) -> o (h t) q", t=NT),
                                     mshift[:, b % 2, i, :]).then_inc(shifted[b], 16)
            for n in range(TILES):
                sp.wait_ge(y_out, n + 1)
                sp.dma_start(out[n * P:(n + 1) * P, :], yout[:, n, :]).then_inc(done, 16)
            sp.wait_ge(done, 16 * TILES)

        @block.gpsimd
        def _(pool):
            pool.dma_start(rows_sb[:, :], rows.partition_broadcast(P)).then_inc(ld_rows, 16)
            count = {}

            def own(ins, signal=pool_done):
                count[signal.name] = count.get(signal.name, 0) + 1
                ins.then_inc(signal, 1)
                pool.wait_ge(signal, count[signal.name])

            own(pool.memset(ident[:, :], 0.0))
            own(pool.memset(ones_row[:, :], 1.0))
            own(pool.memset(maskb[:, :, :], 0.0))
            own(pool.affine_select(out=ident[:, :], in_=ident[:, :], compare_op=ALU.not_equal, fill=1.0, base=0,
                                   pattern=[[-1, P]], channel_multiplier=1))
            own(pool.affine_select(out=maskb[:, :, :], in_=maskb[:, :, :], compare_op=ALU.is_ge, fill=SHUT, base=0,
                                   pattern=[[0, 4], [-1, P]], channel_multiplier=1))
            own(pool.tensor_copy(identb[:, :], ident[:, :]), consts)
            for b in range(KBUF):
                own(pool.memset(qx[64:P, b, :, :].bitcast(U32), 0), zeroed)
                own(pool.memset(kx[64:P, b, :, :].bitcast(U32), 0))
                own(pool.memset(kx[MROW:MROW + 2, b, :, :], 1.0), zeroed)
                if b == 0:
                    own(pool.iota(delta[:, :], pattern=[[1, S]], base=0, channel_multiplier=-1))
                    own(pool.tensor_copy(deltaf[:, :], delta[:, :]))
                    own(pool.tensor_scalar(deltaf[:, :], deltaf[:, :], 1.0, None, ALU.max))
                    own(pool.memset(decay[:, :], -DECAY))
                    own(pool.tensor_tensor(decay[:, :], deltaf[:, :], decay[:, :], ALU.pow))
                    own(pool.affine_select(out=decay[:, :], in_=decay[:, :], compare_op=ALU.is_ge, fill=0.0, base=0,
                                           pattern=[[1, S]], channel_multiplier=-1), decay_ready)
                    own(pool.memset(mhalf[:, :], -0.5))
                    own(pool.iota(rank8i[:, :], pattern=[[-1, E]], base=E, channel_multiplier=0))
                    own(pool.tensor_copy(rank8[:, :], rank8i[:, :]), consts)
                    pool.wait_ge(ld_x, 16)
                    pool.wait_ge(ld_rows, 16)
                    own(pool.tensor_tensor(xb[:, :, :], x_sb[:, :, :],
                                           R(BO).unsqueeze(1).to_broadcast([P, TILES, D]), ALU.add), xb_ready)
            norms = 0
            for kind, b, u in order:
                if kind == "exp" and u == NU - 1 and b + KBUF < B:
                    filled(pool, "s", (kind, b, u))
                    own(pool.memset(qx[MROW:MROW + 2, b % KBUF, :, :].bitcast(U32), 0), zeroed)
                if kind in ("out", "cross"):
                    norms += 1
                    pool.wait_ge(var_ready, norms)
                    own(pool.tensor_tensor(rstd[:, :], var[:, :], mhalf[:, 0:NT], ALU.pow), rstd_ready)
            for _ in range(2):
                norms += 1
                pool.wait_ge(var_ready, norms)
                own(pool.tensor_tensor(rstd4[:, :], var4[:, :], mhalf[:, 0:4], ALU.pow), rstd_ready)

        @block.scalar
        def _(act):
            act.wait_ge(ld_x0, 48)
            act.activation(bqs[:, :], cols_sb[:, BQ:BQ + 1], ACT.Copy, scale=float(DK) ** -0.5).then_inc(qk_ready, 1)
            act.wait_ge(qk_ready, 1)
            n_sc = 0
            for piece in order:
                kind, b, u = piece
                if kind == "proj":
                    qk, free = filled(act, "m", piece, 0)
                    if b >= 2:
                        act.wait_ge(parts_ready, b - 1)
                    act.activation(qk32[:, b % 2, 0:S], qk[:, 0:S], ACT.Identity, bias=bqs[:, :],
                                   scale=float(DK) ** -0.5)
                    act.activation(qk32[:, b % 2, S:2 * S], qk[:, S:2 * S], ACT.Identity,
                                   bias=cols_sb[:, BK:BK + 1]).then_inc(free, 1)
                if kind == "ctx":
                    k2, free = filled(act, "m", piece, 0)
                    if b >= KBUF:
                        filled(act, "s", ("relu", b - KBUF, 0))
                    act.activation(k2T[:, b % KBUF, :], k2[:, :], ACT.Identity, bias=cols_sb[:, XBK:XBK + 1]).then_inc(free, 1)
                if kind == "shift":
                    mt, _f = filled(act, "m", piece)
                    if b >= 2:
                        act.wait_ge(shifted[b - 2], 32)
                    act.activation(mshift[:, b % 2, 0, :], mt[0:2 * H, 0:P], ACT.Copy, scale=-1.0).then_inc(mhi_ready, 1)
                if kind == "exp":
                    sc, free = filled(act, "s", piece)
                    k = NU * b + u
                    if k >= EBUF:
                        ob, ou = divmod(k - EBUF, NU)
                        act.wait_ge(pv_done, 4 * ob + (2 if ou < 3 else 4))
                    act.activation(es[:, k % EBUF, :], sc[:, :], ACT.Exp).then_inc(free, 1)
                if kind == "evac":
                    act.wait_ge(pv_done, 4 * b + 4)
                    if b:
                        act.wait_ge(turned, b)
                    act.activation(osb[:, 0:2, :], ps_o[:, 0:512].rearrange("p (g q) -> p g q", g=2), ACT.Copy)
                    act.activation(osb[:, 2:4, :], ps_o[:, 512:1024].rearrange("p (g q) -> p g q", g=2),
                                   ACT.Copy).then_inc(osb_ready, 1)
                if kind == "back":
                    at, free = filled(act, "m", piece)
                    act.activation(attnT[:, :], at[:, 0:S], ACT.Copy).then_inc(free, 1)
                if kind == "x1t":
                    at, free = filled(act, "m", piece)
                    act.activation(x1T[:, :], at[:, 0:S], ACT.Copy).then_inc(free, 1)
                if kind == "q2":
                    at, free = filled(act, "m", piece)
                    act.activation(q2T[:, :], at[:, 0:S], ACT.Identity, bias=cols_sb[:, XBQ:XBQ + 1]).then_inc(free, 1)
                if kind == "relu":
                    at, free = filled(act, "s", piece)
                    act.activation(sc2[:, :, :], at[:, :].rearrange("p (k q) -> p k q", k=KT), ACT.Relu).then_inc(free, 1)
                if kind == "x2t":
                    at, free = filled(act, "m", piece)
                    act.activation(x2T[:, b * S:(b + 1) * S], at[:, 0:S], ACT.Copy).then_inc(free, 1)
            act.wait_ge(ld_ffn, 64)
            s_at = used["s"]
            for half in range(2):
                for e in range(E):
                    i = half * E + e
                    for c in range(0, FC, 2):
                        k = s_at
                        s_at += 1
                        act.wait_ge(s_full[k % 2], k // 2 + 1)
                        if i >= 2 and c == 0:
                            m = used["m"] + i - 2
                            act.wait_ge(m_full[m % 2], m // 2 + 1)
                        for cc in range(2):
                            ins = act.activation(hT[:, i % 2, c + cc, :], ps_s[k % 2][:, cc * 512:(cc + 1) * 512], ACT.Relu,
                                                 bias=b1_sb[:, e * FC + c + cc:e * FC + c + cc + 1])
                        ins.then_inc(s_free[k % 2], 1)

        @block.tensor
        def _(pe):
            pe.wait_ge(ld_x0, 48)
            for piece in order:
                kind, b, u = piece
                if kind == "proj":
                    if b == 1:
                        pe.wait_ge(ld_xT, 16)
                    xTb = xT_sb[:, b * S:(b + 1) * S]
                    qk, full = vacant(pe, "m", piece, 0)
                    pe.matmul(qk[:, 0:S], W(WQ), xTb, start=True, stop=True)
                    pe.matmul(qk[:, S:2 * S], W(WK), xTb, start=True, stop=True).then_inc(full, 1)
                    v, full = vacant(pe, "m", piece, 1)
                    for t in range(NT):
                        mm = pe.matmul(v[:, t * D:(t + 1) * D], xTb[:, t * P:(t + 1) * P], W(WV), start=True, stop=True)
                    mm.then_inc(full, 1)
                if kind == "ctx":
                    if b == 0:
                        pe.wait_ge(ld_ctx, 16)
                        pe.wait_ge(ld_w, 16)
                    cT = ctxT_sb[:, b * SK:(b + 1) * SK]
                    k2, full = vacant(pe, "m", piece, 0)
                    pe.matmul(k2[:, :], W(XK), cT, start=True, stop=True).then_inc(full, 1)
                    v, full = vacant(pe, "m", piece, 1)
                    for t in range(KT):
                        mm = pe.matmul(v[:, t * D:(t + 1) * D], cT[:, t * P:(t + 1) * P], W(XV), start=True, stop=True)
                    mm.then_inc(full, 1)
                if kind == "max":
                    if u == 0:
                        pe.wait_ge(spread[b], 16 * 18)
                        pe.wait_ge(zeroed, min(2 * b + 2, B + KBUF))
                        if b == 0:
                            pe.wait_ge(consts, 1)
                    sc, full = vacant(pe, "s", piece)
                    t, h0, _n = max_unit(u)
                    keys = (t + 1) * P
                    hs = 512 // keys
                    for bank in range(2):
                        o = sc[:, bank * 512:(bank + 1) * 512].rearrange("p (h k) -> p h k", h=hs)
                        pe.matmul(o[:, :, t * P:keys], identb[:, :], maskb[:, 0:hs, :], start=True, stop=False,
                                  skip_group_check=True)
                        for j in range(hs):
                            h = h0 + bank * hs + j
                            mm = pe.matmul(o[:, j, :], qx[:, b % KBUF, h, t * P:(t + 1) * P], kx[:, b % KBUF, h, 0:keys],
                                           start=False, stop=(j == hs - 1), skip_group_check=True)
                    mm.then_inc(full, 1)
                if kind == "shift":
                    for last in (NU - 2, NU - 1):
                        taken(pe, "s", ("max", b, last))
                    mt, full = vacant(pe, "m", piece)
                    pe.transpose(mt[0:2 * H, 0:P], mx[:, b % 2, :, :].rearrange("p h t -> p (h t)"),
                                 ident[:, :]).then_inc(full, 1)
                if kind == "exp":
                    if u == 0:
                        pe.wait_ge(shifted[b], 32)
                    sc, full = vacant(pe, "s", piece)
                    kt, h0, n = UNITS[u]
                    qs = S - kt * P
                    for j in range(n):
                        h = h0 + j
                        mm = pe.matmul(sc[:, j * qs:(j + 1) * qs], kx[:, b % KBUF, h, kt * P:(kt + 1) * P],
                                       qx[:, b % KBUF, h, kt * P:S], start=True, stop=True)
                    mm.then_inc(full, 1)
                if kind == "pv":
                    pe.wait_ge(p_ready, NU * b + (3 if u < 2 else 6))
                    if u == 0:
                        taken(pe, "m", ("proj", b, 0), 1)
                        if b:
                            pe.wait_ge(attn_ready, b)
                    for kt in range(NT):
                        for j in range(4):
                            h = 4 * u + j
                            k, at = where(kt, h)
                            qs = S - kt * P
                            mm = pe.matmul(ps_o[VW * j:VW * (j + 1), u * S + kt * P:(u + 1) * S], vx[:, b % KBUF, kt, h, :],
                                           es[:, (NU * b + k) % EBUF, at:at + qs], start=(kt == 0), stop=(kt == 1))
                    mm.then_inc(pv_done, 1)
                if kind == "turn":
                    pe.wait_ge(osb_ready, b + 1)
                    for t in range(NT):
                        for g in range(4):
                            mm = pe.transpose(ps_o[:, t * 512 + g * P:t * 512 + (g + 1) * P],
                                              osb[:, g, t * P:(t + 1) * P], ident[:, :])
                    mm.then_inc(turned, 1)
                if kind == "back":
                    pe.wait_ge(attn_ready, b + 1)
                    at, full = vacant(pe, "m", piece)
                    for t in range(NT):
                        mm = pe.transpose(at[:, t * P:(t + 1) * P], attn[:, t, :], ident[:, :])
                    mm.then_inc(full, 1)
                if kind == "out":
                    taken(pe, "m", ("back", b, 0))
                    y, full = vacant(pe, "m", piece)
                    for t in range(NT):
                        mm = pe.matmul(y[:, t * D:(t + 1) * D], attnT[:, t * P:(t + 1) * P], W(WO), start=True, stop=True)
                    mm.then_inc(full, 1)
                if kind == "x1t":
                    pe.wait_ge(x1_ready, b + 1)
                    at, full = vacant(pe, "m", piece)
                    for t in range(NT):
                        mm = pe.transpose(at[:, t * P:(t + 1) * P], x1[:, b * NT + t, :], ident[:, :])
                    mm.then_inc(full, 1)
                if kind == "q2":
                    taken(pe, "m", ("x1t", b, 0))
                    at, full = vacant(pe, "m", piece)
                    pe.matmul(at[:, 0:S], W(XQ), x1T[:, :], start=True, stop=True).then_inc(full, 1)
                if kind == "relu":
                    taken(pe, "m", ("q2", b, 0))
                    taken(pe, "m", ("ctx", b, 0))
                    at, full = vacant(pe, "s", piece)
                    for k in range(KT):
                        mm = pe.matmul(at[:, k * S:(k + 1) * S], k2T[:, b % KBUF, k * P:(k + 1) * P], q2T[:, :],
                                       start=True, stop=True)
                    mm.then_inc(full, 1)
                if kind == "cross":
                    taken(pe, "s", ("relu", b, 0))
                    taken(pe, "m", ("ctx", b, 0), 1)
                    at, full = vacant(pe, "m", piece)
                    for t in range(NT):
                        for k in range(KT):
                            mm = pe.matmul(at[:, t * D:(t + 1) * D], sc2[:, k, t * P:(t + 1) * P], v2[:, b % KBUF, k, :],
                                           start=(k == 0), stop=(k == KT - 1))
                    mm.then_inc(full, 1)
                if kind == "x2t":
                    pe.wait_ge(x2_ready, b + 1)
                    at, full = vacant(pe, "m", piece)
                    for t in range(NT):
                        mm = pe.transpose(at[:, t * P:(t + 1) * P], x2[:, b * NT + t, :], ident[:, :])
                    mm.then_inc(full, 1)
                if kind == "route":
                    taken(pe, "m", ("x2t", b, 0))
                    at, full = vacant(pe, "m", piece)
                    for t in range(NT):
                        mm = pe.matmul(at[:, t * E:(t + 1) * E], x2T[:, b * S + t * P:b * S + (t + 1) * P], W(WR),
                                       start=True, stop=True)
                    mm.then_inc(full, 1)
            pe.wait_ge(ld_ffn, 64)
            s_at, m_at = used["s"], used["m"]
            for half in range(2):
                for e in range(E):
                    i = half * E + e
                    for c in range(0, FC, 2):
                        k = s_at
                        s_at += 1
                        pe.wait_ge(s_free[k % 2], k // 2)
                        for cc in range(2):
                            mm = pe.matmul(ps_s[k % 2][:, cc * 512:(cc + 1) * 512], w1_sb[:, e, (c + cc) * P:(c + cc + 1) * P],
                                           x2T[:, half * 512:(half + 1) * 512], start=True, stop=True)
                        mm.then_inc(s_full[k % 2], 1)
                    k = m_at
                    m_at += 1
                    pe.wait_ge(m_free[k % 2], k // 2)
                    for q in (1, 2):
                        pe.wait_ge(s_free[(s_at - q) % 2], (s_at - q) // 2 + 1)
                    for t in range(4):
                        pe.matmul(ps_m[k % 2][:, t * D:(t + 1) * D], ones_row[:, :], b2_sb[:, e, :], start=True, stop=False)
                        for c in range(FC):
                            mm = pe.matmul(ps_m[k % 2][:, t * D:(t + 1) * D], hT[:, i % 2, c, t * P:(t + 1) * P],
                                           w2_sb[:, e, c, :], start=False, stop=(c == FC - 1))
                    mm.then_inc(m_full[k % 2], 1)

        @block.vector
        def _(v):
            link = [0]

            def own(ins):
                link[0] += 1
                ins.then_inc(dve, 1)
                v.wait_ge(dve, link[0])

            norms = [0]

            def layer_norm(dst, ready):
                for t in range(NT):
                    ins = v.bn_stats(stats[:, t, :], z[:, t, :])
                own(ins)
                for t in range(NT):
                    ins = v.bn_aggr(mv[:, t, :], stats[:, t, :])
                own(ins)
                norms[0] += 1
                v.tensor_scalar(var[:, :], mv[:, :, 1], EPS, None, ALU.add).then_inc(var_ready, 1)
                v.wait_ge(rstd_ready, norms[0])
                for t in range(NT):
                    ins = v.tensor_scalar(dst[:, t, :], z[:, t, :], mv[:, t, 0:1], rstd[:, t:t + 1],
                                          ALU.subtract, ALU.mult)
                ins.then_inc(ready, 1)

            v.memset(vx[:, :, :, :, :].rearrange("p b t h w -> p (b t h) w")[:, :, DK + 1:VW], 0.0)
            v.memset(vx[:, :, :, :, :].rearrange("p b t h w -> p (b t h) w")[:, :, DK:DK + 1], 1.0)
            v.wait_ge(consts, 2)
            for piece in order:
                kind, b, u = piece
                if kind == "proj":
                    taken(v, "m", piece)
                    if b >= 2:
                        v.wait_ge(stored[b - 2], 16)
                    q, r = qk32[:, b % 2, :], rest[:, b % 2, :]
                    p = [parts[:, b % 2, i, :] for i in range(PARTS)]
                    own(v.tensor_copy(p[0], q))
                    own(v.tensor_tensor(r, q, p[0], ALU.subtract))
                    own(v.tensor_copy(p[1], r))
                    v.tensor_tensor(p[2], r, p[1], ALU.subtract).then_inc(parts_ready, 1)
                    vp, free = filled(v, "m", piece, 1)
                    v.wait_ge(ld_rows, 16)
                    if b >= KBUF:
                        v.wait_ge(pv_done, 4 * (b - KBUF + 1))
                    for t in range(NT):
                        ins = v.tensor_tensor(vx[:, b % KBUF, t, :, 0:DK],
                                              vp[:, t * D:(t + 1) * D].rearrange("p (h d) -> p h d", h=H),
                                              R(BV).rearrange("p (h d) -> p h d", h=H), ALU.add)
                        if t == 0:
                            own(ins)
                    ins.then_inc(free, 1)
                if kind == "ctx":
                    vp, free = filled(v, "m", piece, 1)
                    v.wait_ge(ld_rows, 16)
                    if b >= KBUF:
                        filled(v, "m", ("cross", b - KBUF, 0))
                    v.tensor_tensor(v2[:, b % KBUF, :, :], vp[:, :].rearrange("p (k d) -> p k d", k=KT),
                                    R(XBV).unsqueeze(1).to_broadcast([P, KT, D]), ALU.add).then_inc(free, 1)
                if kind == "max":
                    sc, free = filled(v, "s", piece)
                    t, h0, n = max_unit(u)
                    keys = (t + 1) * P
                    if u == 0 and b >= 2:
                        filled(v, "m", ("shift", b - 2, 0))
                    v.tensor_reduce(mx[:, b % 2, h0:h0 + n, t], sc[:, :].rearrange("p (h k) -> p h k", h=n), AX.X,
                                    ALU.max).then_inc(free, 1)
                if kind == "shift":
                    mt, free = filled(v, "m", piece)
                    v.wait_ge(mhi_ready, b + 1)
                    v.scalar_tensor_tensor(out=mshift[:, b % 2, 1, :], in0=mt[0:2 * H, 0:P], scalar=-1.0,
                                           in1=mshift[:, b % 2, 0, :], op0=ALU.mult, op1=ALU.subtract).then_inc(free, 1)
                if kind == "exp":
                    taken(v, "s", piece)
                    if b == 0:
                        v.wait_ge(decay_ready, 1)
                    kt, h0, nh = UNITS[u]
                    qs = S - kt * P
                    e = es[:, (NU * b + u) % EBUF, :].rearrange("p (h q) -> p h q", h=nh)
                    v.scalar_tensor_tensor(out=e, in0=e, scalar=CEIL, in1=decay[:, 0:qs].unsqueeze(1).to_broadcast([P, nh, qs]),
                                           op0=ALU.min, op1=ALU.mult).then_inc(p_ready, 1)
                if kind == "turn":
                    v.wait_ge(turned, b + 1)
                    o = ps_o[:, :].rearrange("p (t h w) -> p t h w", t=NT, h=H)
                    if b:
                        filled(v, "m", ("back", b - 1, 0))
                    for t in range(NT):
                        ins = v.reciprocal(rden[:, t, :], o[:, t, :, DK])
                    own(ins)
                    for t in range(NT):
                        ins = v.tensor_tensor(attn[:, t, :].rearrange("p (h d) -> p h d", h=H), o[:, t, :, 0:DK],
                                              rden[:, t, :].unsqueeze(2).to_broadcast([P, H, DK]), ALU.mult)
                        if t == 0:
                            own(ins)
                    ins.then_inc(attn_ready, 1)
                if kind == "out":
                    y, free = filled(v, "m", piece)
                    if b == 0:
                        v.wait_ge(xb_ready, 1)
                    else:
                        v.wait_ge(x2_ready, b)
                    ins = v.tensor_tensor(z[:, :, :], y[:, 0:NT * D].rearrange("p (t d) -> p t d", t=NT),
                                          xb[:, b * NT:(b + 1) * NT, :], ALU.add)
                    ins.then_inc(free, 1)
                    taken(v, "m", piece)
                    layer_norm(x1[:, b * NT:(b + 1) * NT, :], x1_ready)
                if kind == "cross":
                    y, free = filled(v, "m", piece)
                    v.wait_ge(x1_ready, b + 1)
                    ins = v.tensor_tensor(z[:, :, :], y[:, 0:NT * D].rearrange("p (t d) -> p t d", t=NT),
                                          x1[:, b * NT:(b + 1) * NT, :], ALU.add)
                    ins.then_inc(free, 1)
                    taken(v, "m", piece)
                    layer_norm(x2[:, b * NT:(b + 1) * NT, :], x2_ready)
                if kind == "route":
                    at, free = filled(v, "m", piece)
                    hb = hot[:, b * NT:(b + 1) * NT, :]
                    if b:
                        v.wait_ge(hot_ready, b)
                    v.tensor_tensor(lg[:, :, :], at[:, 0:NT * E].rearrange("p (t e) -> p t e", t=NT),
                                    R(BR).unsqueeze(1).to_broadcast([P, NT, E]), ALU.add).then_inc(free, 1)
                    taken(v, "m", piece)
                    own(v.tensor_reduce(lgmax[:, :], lg[:, :, :], AX.X, ALU.max))
                    own(v.tensor_tensor(hb, lg[:, :, :], lgmax[:, :].unsqueeze(2).to_broadcast([P, NT, E]), ALU.is_ge))
                    own(v.tensor_tensor(lg[:, :, :], hb, rank8[:, :].unsqueeze(1).to_broadcast([P, NT, E]), ALU.mult))
                    own(v.tensor_reduce(lgmax[:, :], lg[:, :, :], AX.X, ALU.max))
                    v.tensor_tensor(hb, lg[:, :, :], lgmax[:, :].unsqueeze(2).to_broadcast([P, NT, E]),
                                    ALU.is_equal).then_inc(hot_ready, 1)
            v.wait_ge(hot_ready, B)
            v.wait_ge(x2_ready, B)
            m_at = used["m"]
            for half in range(2):
                for e in range(E):
                    k = m_at
                    m_at += 1
                    v.wait_ge(m_full[k % 2], k // 2 + 1)
                    for t in range(4):
                        n = half * 4 + t
                        src = x2 if e == 0 else acc
                        ins = v.scalar_tensor_tensor(out=acc[:, n, :], in0=ps_m[k % 2][:, t * D:(t + 1) * D],
                                                     scalar=hot[:, n, e:e + 1], in1=src[:, n, :], op0=ALU.mult, op1=ALU.add)
                    ins.then_inc(m_free[k % 2], 1)
                    v.wait_ge(m_free[k % 2], k // 2 + 1)
                for t in range(4):
                    own(v.bn_stats(stats4[:, t, :], acc[:, half * 4 + t, :]))
                    own(v.bn_aggr(mv4[:, t, :], stats4[:, t, :]))
                norms[0] += 1
                v.tensor_scalar(var4[:, :], mv4[:, :, 1], EPS, None, ALU.add).then_inc(var_ready, 1)
                v.wait_ge(rstd_ready, norms[0])
                for t in range(4):
                    n = half * 4 + t
                    v.tensor_scalar(yout[:, n, :], acc[:, n, :], mv4[:, t, 0:1], rstd4[:, t:t + 1],
                                    ALU.subtract, ALU.mult).then_inc(y_out, 1)


def max_unit(u):
    return (0, 8 * u, 8) if u < 2 else (1, 4 * (u - 2), 4)


def where(kt, h):
    for k, (t, h0, n) in enumerate(UNITS):
        if t == kt and h0 <= h < h0 + n:
            return k, (h - h0) * (S - kt * P)


def kernel(**inputs):
    import numpy as np
    import concourse.bacc as bacc
    from concourse.bass_utils import run_bass_kernel_spmd as run

    a = {k: np.asarray(v) for k, v in inputs.items()}
    arrays = {
        "xtok": a["x"].reshape(B * S, D),
        "xT": a["x"].reshape(B * S, D).T,
        "ctxT": a["ctx_1024"].reshape(B * SK, D).T,
        "wts": np.concatenate([a["L0_attn_Wq"], a["L0_attn_Wk"], a["L0_attn_Wv"], a["L0_attn_Wo"], a["L0_xattn_Wq"].T,
                               a["L0_xattn_Wk"].T, a["L0_xattn_Wv"].T, a["L0_ffn_Wr"].T], axis=1),
        "cols": np.stack([a["L0_attn_bq"], a["L0_attn_bk"], a["L0_xattn_bq"], a["L0_xattn_bk"]], axis=1),
        "rows": np.concatenate([a["L0_attn_bv"], a["L0_attn_bo"], a["L0_xattn_bv"], a["L0_ffn_br"]]),
        "w1T": a["L0_ffn_W1"].transpose(2, 0, 1).reshape(D, E * FF),
        "w2T": a["L0_ffn_W2"].reshape(E, D, FC, P).transpose(3, 0, 2, 1).reshape(P, E * FC * D),
        "b1c": a["L0_ffn_b1"].reshape(E, FC, P).transpose(2, 0, 1).reshape(P, E * FC),
        "b2r": a["L0_ffn_b2"],
    }
    nc = bacc.Bacc("TRN2", target_bir_lowering=False, num_devices=1)
    args = []
    for name, v in arrays.items():
        arrays[name] = np.ascontiguousarray(v)
        args.append(nc.dram_tensor(name, v.shape, mybir.dt.from_np(v.dtype), kind="ExternalInput").ap())
    args.append(nc.dram_tensor("out", (B * S, D), F32, kind="ExternalOutput").ap())
    decoder_kernel(nc, *args)
    r = run(nc, [arrays], core_ids=[0])
    return r.results[0]["out"].reshape(B, S, D)
```

```python
from contextlib import ExitStack

import concourse.bass as bass
from concourse import mybir

F32 = mybir.dt.float32
BF16 = mybir.dt.bfloat16
I32 = mybir.dt.int32
U32 = mybir.dt.uint32
ALU = mybir.AluOpType
ACT = mybir.ActivationFunctionType
AX = mybir.AxisListType

P = 128
B, S, D = 4, 256, 128
NT = S // P
TILES = B * NT
H = 16
DK = D // H
SK = 512
KT = SK // P
E, FF = 8, 512
FC = FF // P
PARTS = 3
TERM = PARTS * PARTS * DK
MROW = 96
VW = 32
EPS = 1e-5
DECAY = 0.25
REGION = B * S + P
ROWS = E * REGION + P
LATE = S // P + 1
XW = D + 4
NOBODY = 1 << 20
FT = (B * S - E) // P + E
FTP = 16
WBUF = 6
ONES2 = 0x3F803F80
SHUT = -1e30
CEIL = 1e30

UNITS = [(0, 0, 4), (0, 4, 4), (1, 0, 8), (0, 8, 4), (0, 12, 4), (1, 8, 8)]
NU = len(UNITS)
KBUF = 3
EBUF = 7


ROUND = [("pv", -1, 2), ("pv", -1, 3), ("evac", -1, 0), ("max", 1, 0), ("max", 1, 1), ("turn", -1, 0),
         ("max", 1, 2), ("x2t", -2, 0), ("rank", -3, 0), ("max", 1, 3), ("back", -1, 0), ("out", -1, 0),
         ("exp", 0, 0), ("norm1", -1, 0), ("proj", 2, 0), ("exp", 0, 1), ("exp", 0, 2), ("exp", 0, 3),
         ("x1t", -1, 0), ("exp", 0, 4), ("q2", -1, 0), ("exp", 0, 5), ("relu", -1, 0), ("max", 1, 4),
         ("pv", 0, 0), ("max", 1, 5), ("route", -2, 0), ("pv", 0, 1), ("cross", -1, 0), ("ctx", 2, 0),
         ("norm2", -1, 0), ("shift", 1, 0)]


def schedule():
    out = [("proj", 0, 0), ("proj", 1, 0), ("ctx", 0, 0), ("ctx", 1, 0)]
    out += [("max", 0, u) for u in range(NU)] + [("shift", 0, 0)]
    for r in range(B + 3):
        out += [(kind, r + rel, u) for kind, rel, u in ROUND if 0 <= r + rel < B and (r > 0 or rel >= 0)]
    return out


def expert_schedule():
    out = [("gather", 0, 0), ("gather", 1, 0), ("up", 0, 0)]
    for i in range(1, FT + 1):
        out += [("gather", i + 1, 0), ("up", i, 0), ("down", i - 1, 0)]
    return [p for p in out if p[1] < FT]


USES = {"proj": "mm", "ctx": "mm", "max": "s", "shift": "m", "exp": "s", "back": "m", "out": "m",
        "x1t": "m", "q2": "m", "relu": "s", "cross": "m", "x2t": "m", "route": "m", "rank": "m",
        "gather": "m", "up": "s", "down": "m"}


def slots(order):
    at = {"s": 0, "m": 0}
    out = {}
    for piece in order:
        for j, ring in enumerate(USES.get(piece[0], "")):
            out[(*piece, j)] = (at[ring] % 2, at[ring] // 2)
            at[ring] += 1
    return out


def decoder_kernel(nc, xtok, xT, ctxT, wts, cols, rows, w1T, w2T, b1c, b2r, tables, out):
    order, tiles = schedule(), expert_schedule()
    place = slots(order + tiles)
    norm_at = {p: n + 1 for n, p in enumerate(q for q in order if q[0] in ("out", "cross"))}
    WQ, WK, WV, WO, XQ, XK, XV, WR = range(8)
    BQ, BK, XBQ, XBK, BV = range(5)
    BO, XBV, BR = range(3)

    parts_dram = nc.dram_tensor("parts_dram", [B, 1 + PARTS, D, PARTS * S], BF16, kind="Internal").ap()

    sorted_dram = nc.dram_tensor("sorted_dram", [ROWS, XW], F32, kind="Internal").ap()

    with ExitStack() as ctx:
        def sb(name, shape, dt=F32):
            return ctx.enter_context(nc.sbuf_tensor(name, shape, dt))

        def psum(name, cols_):
            return ctx.enter_context(nc.psum_tensor(name, [P, cols_], F32))

        def sem(name):
            return ctx.enter_context(nc.semaphore(name))

        w_sb = sb("w_sb", [P, 7 * D + E])
        cols_sb = sb("cols_sb", [P, 5])
        rows_sb = sb("rows_sb", [P, 2 * D + E])
        xT_sb = sb("xT_sb", [P, B * S])
        x_sb = sb("x_sb", [P, TILES, D])
        ctxT_sb = sb("ctxT_sb", [P, B * SK])
        w2_sb = sb("w2_sb", [P, E, FC, D])
        b1_sb = sb("b1_sb", [P, E * FC])
        b2_sb = sb("b2_sb", [P, E, D])
        tab_sb = sb("tab_sb", [P, NTAB])

        def W(i):
            return w_sb[:, i * D:(i + 1) * D] if i < WR else w_sb[:, WR * D:WR * D + E]

        def R(i):
            return rows_sb[:, i * D:(i + 1) * D] if i < BR else rows_sb[:, BR * D:BR * D + E]

        ident = sb("ident", [P, P])
        identb = sb("identb", [P, P], BF16)
        maskb = sb("maskb", [P, 4, P], BF16)
        before = sb("before", [P, P], BF16)
        onesb = sb("onesb", [P, P], BF16)
        blank = sb("blank", [P, XW])
        mhalf = sb("mhalf", [P, 16])
        bqs = sb("bqs", [P, 1])

        decay = tab_sb[:, 0:S]
        rank8 = tab_sb[:, S:S + E]
        region = tab_sb[:, S + E:S + 2 * E]
        fills = tab_sb[0:1, S + 2 * E:S + 3 * E]
        lower = tab_sb[0:1, S + 3 * E:S + 3 * E + E * E].rearrange("p (a b) -> p a b", a=E)
        number = tab_sb[0:1, S + 3 * E + E * E:S + 3 * E + E * E + FTP * E].rearrange("p (i e) -> p i e", e=E)

        qk32 = sb("qk32", [P, 2, 2, S])
        rest = sb("rest", [P, 2, 2, S])
        parts = sb("parts", [P, 2, 2 * PARTS - 1, 2, S], BF16)
        qx = sb("qx", [P, KBUF, H, S], BF16)
        kx = sb("kx", [P, KBUF, H, S], BF16)
        vx = sb("vx", [P, KBUF, NT, H, VW])
        mx = sb("mx", [P, 2, H, NT])
        mshift = sb("mshift", [2 * H, 2, 2, P], BF16)
        es = sb("es", [P, EBUF, 1024])
        osb = sb("osb", [P, 4, S])
        rden = sb("rden", [P, NT, H])
        attn = sb("attn", [P, NT, D])
        attnT = sb("attnT", [P, S])
        xb = x_sb
        z = [sb(f"z{k}", [P, NT, D]) for k in range(2)]
        stats = sb("stats", [P, NT, 6])
        mv = sb("mv", [P, 2, NT, 2])
        rstd = sb("rstd", [P, 2, NT])
        var = sb("var", [P, 2, NT])
        x1 = sb("x1", [P, TILES, D])
        x1T = sb("x1T", [P, S])
        q2T = sb("q2T", [P, S])
        k2T = sb("k2T", [P, KBUF, SK])
        v2 = sb("v2", [P, KBUF, KT, D])
        sc2 = sb("sc2", [P, KT, S])
        x2 = sb("x2", [P, TILES, XW])
        x2T = sb("x2T", [P, S])
        lg = sb("lg", [P, NT, E])
        lgmax = sb("lgmax", [P, NT])
        hot = sb("hot", [P, NT, E])
        hotb = sb("hotb", [P, TILES, E], BF16)
        slotf = sb("slotf", [P, NT])
        regionb = sb("regionb", [1, E], BF16)
        slot32 = sb("slot32", [P, TILES], I32)
        total = sb("total", [1, E])
        more = sb("more", [1, E, E])
        ntile = sb("ntile", [1, E])
        ends = sb("ends", [1, E])
        past = sb("past", [1, FTP, E])
        past2 = sb("past2", [1, FTP, E])
        texp = sb("texp", [1, FTP])
        tfirst = sb("tfirst", [1, FTP])
        end32 = sb("end32", [1, E], I32)
        trow32 = sb("trow32", [1, FTP], I32)
        texp32 = sb("texp32", [1, FTP], I32)
        room = es[:, :, :].rearrange("p k n -> p (k n)")
        w1_t = [room[:, k * FF:(k + 1) * FF] for k in range(WBUF)]
        at = WBUF * FF
        hT = [room[:, at + k * FF:at + (k + 1) * FF] for k in range(2)]
        at += 2 * FF
        xsT = [room[:, at + k * P:at + (k + 1) * P] for k in range(2)]
        at += 2 * P
        zt = [room[:, at + k * D:at + (k + 1) * D] for k in range(2)]
        at += 2 * D
        xres = [room[:, at + k * D:at + (k + 1) * D] for k in range(2)]
        token_room = qx[:, :, :, :].rearrange("p b h t -> p (b h t)").bitcast(F32)
        xt = [token_room[:, i * XW:(i + 1) * XW] for i in range(FT)]
        yo = [token_room[:, FT * XW + i * D:FT * XW + (i + 1) * D] for i in range(FT)]
        st = [stats[:, k, :] for k in range(2)]

        ps_s = [psum(f"ps_s{i}", 1024) for i in range(2)]
        ps_m = [psum(f"ps_m{i}", 512) for i in range(2)]
        ps_o = psum("ps_o", 1024)

        s_full = [sem(f"s_full{i}") for i in range(2)]
        s_free = [sem(f"s_free{i}") for i in range(2)]
        m_full = [sem(f"m_full{i}") for i in range(2)]
        m_free = [sem(f"m_free{i}") for i in range(2)]
        ring = {"s": (ps_s, s_full, s_free), "m": (ps_m, m_full, m_free)}

        ld_w = sem("ld_w")
        ld_rows = sem("ld_rows")
        ld_x0 = sem("ld_x0")
        ld_xT = sem("ld_xT")
        ld_x = sem("ld_x")
        ld_ctx = sem("ld_ctx")
        ld_ffn = sem("ld_ffn")
        stored = [sem(f"stored{b}") for b in range(B)]
        spread = [sem(f"spread{b}") for b in range(B)]
        shifted = [sem(f"shifted{b}") for b in range(B)]
        pool_done = sem("pool_done")
        consts = sem("consts")
        zeroed = sem("zeroed")
        xb_ready = sem("xb_ready")
        dve = sem("dve")
        var_ready = sem("var_ready")
        rstd_ready = sem("rstd_ready")
        vx_ready = sem("vx_ready")
        first_part = sem("first_part")
        qk_ready = sem("qk_ready")
        parts_ready = sem("parts_ready")
        mhi_ready = sem("mhi_ready")
        exp_ready = sem("exp_ready")
        p_ready = sem("p_ready")
        pv_done = sem("pv_done")
        osb_ready = sem("osb_ready")
        turned = sem("turned")
        attn_ready = sem("attn_ready")
        x1_ready = sem("x1_ready")
        x2_ready = sem("x2_ready")
        hot_ready = sem("hot_ready")
        ranked = sem("ranked")
        blanked = sem("blanked")
        blank_ready = sem("blank_ready")
        placed = sem("placed")
        table_ready = sem("table_ready")
        ld_b2 = sem("ld_b2")
        ld_tab = sem("ld_tab")
        xt_full = [sem(f"xt_full{i}") for i in range(FT)]
        w1_full = [sem(f"w1_full{i}") for i in range(WBUF)]
        ends_ready = sem("ends_ready")
        yo_ready = sem("yo_ready")
        done = sem("done")

        block = ctx.enter_context(nc.Block())

        def filled(eng, name, piece, j=0):
            slot, n = place[(*piece, j)]
            eng.wait_ge(ring[name][1][slot], n + 1)
            return ring[name][0][slot], ring[name][2][slot]

        def taken(eng, name, piece, j=0):
            slot, n = place[(*piece, j)]
            eng.wait_ge(ring[name][2][slot], n + 1)

        def vacant(pe, name, piece, j=0):
            slot, n = place[(*piece, j)]
            if n:
                pe.wait_ge(ring[name][2][slot], n)
            return ring[name][0][slot], ring[name][1][slot]

        @block.sync
        def _(sp):
            sp.dma_start(w_sb[:, 0:3 * D], wts[:, 0:3 * D]).then_inc(ld_x0, 16)
            sp.dma_start(xT_sb[:, 0:S], xT[:, 0:S]).then_inc(ld_x0, 16)
            sp.dma_start(cols_sb[:, :], cols).then_inc(ld_x0, 16)
            sp.dma_start(tab_sb[:, :], tables).then_inc(ld_tab, 16)
            sp.dma_start(xT_sb[:, S:], xT[:, S:]).then_inc(ld_xT, 16)
            sp.dma_start(w_sb[:, 3 * D:], wts[:, 3 * D:]).then_inc(ld_w, 16)
            sp.dma_start(ctxT_sb[:, :], ctxT).then_inc(ld_ctx, 16)
            sp.dma_start(x_sb[:, :, :], xtok.rearrange("(n p) d -> p n d", p=P)).then_inc(ld_x, 16)
            for kind, b, _i in order:
                if kind == "proj":
                    sp.wait_ge(parts_ready, 2 * b + 2)
                    sp.dma_start(parts_dram[b, 0].rearrange("p (i t) -> p i t", i=PARTS), parts[:, b % 2, 0:PARTS, 0, :]).then_inc(stored[b], 16)
                    for c in range(PARTS):
                        sp.dma_start(parts_dram[b, 1 + c].rearrange("p (i t) -> p i t", i=PARTS), parts[:, b % 2, c:c + PARTS, 1, :])\
                            .then_inc(stored[b], 16)
                    sp.wait_ge(stored[b], 16 * (1 + PARTS))
                    sp.wait_ge(zeroed, min(2 * b + 2, B + KBUF))
                    if b >= KBUF:
                        filled(sp, "s", ("exp", b - KBUF, NU - 1))
                    for c in range(PARTS):
                        rows_c = slice(c * PARTS * DK, (c + 1) * PARTS * DK)
                        for x, src in ((qx, 0), (kx, 1 + c)):
                            sp.dma_start(x[rows_c, b % KBUF, :, :], parts_dram[b, src].rearrange(
                                "(h d) (i t) -> (d i) h t", d=DK, i=PARTS)).then_inc(spread[b], 16)
                    if b == 2:
                        sp.dma_start(w2_sb[:, :, :, :],
                                     w2T.rearrange("p (e c d) -> p e c d", e=E, c=FC)).then_inc(ld_ffn, 16)
                        sp.dma_start(b1_sb[:, :], b1c).then_inc(ld_ffn, 16)
                        sp.wait_ge(blank_ready, 1)
                        sp.dma_start(sorted_dram[E * REGION:, :], blank[:, :]).then_inc(blanked, 16)
                if kind == "rank" and b == B - 2:
                    sp.wait_ge(ends_ready, 1)
                    for e in range(E):
                        row = sp.value_load(end32[0:1, e:e + 1], min_val=0, max_val=(E - 1) * REGION + (B - 1) * S)
                        sp.dma_start(sorted_dram[bass.ds(row, LATE * P), :].rearrange("(n p) w -> p n w", p=P),
                                     blank[:, :].unsqueeze(1).to_broadcast([P, LATE, XW])).then_inc(blanked, 16)
                if kind == "shift":
                    taken(sp, "m", ("shift", b, 0))
                    for i in range(2):
                        sp.dma_start(qx[MROW + i:MROW + i + 1, b % KBUF, :, :].rearrange("o h (t q) -> o (h t) q", t=NT),
                                     mshift[:, b % 2, i, :]).then_inc(shifted[b], 16)
            sp.wait_ge(table_ready, 2)

            def load_w1(i):
                if i >= WBUF:
                    filled(sp, "s", ("up", i - WBUF, 0))
                e = sp.value_load(texp32[0:1, i:i + 1], min_val=0, max_val=E - 1)
                sp.dma_start(w1_t[i % WBUF].rearrange("p (a f) -> p a f", a=1),
                             w1T.rearrange("p (e f) -> p e f", e=E)[:, bass.ds(e, 1), :]).then_inc(w1_full[i % WBUF], 16)

            for i in range(2):
                load_w1(i)
            sp.wait_ge(placed, 16 * TILES)
            for i in range(FT):
                row = sp.value_load(trow32[0:1, i:i + 1], min_val=0, max_val=E * REGION)
                sp.dma_start(xt[i], sorted_dram[bass.ds(row, P), :]).then_inc(xt_full[i], 16)
                if i + 2 < FT:
                    load_w1(i + 2)

        @block.gpsimd
        def _(pool):
            pool.dma_start(rows_sb[:, :], rows.partition_broadcast(P)).then_inc(ld_rows, 16)
            count = {}

            def own(ins, signal=pool_done):
                count[signal.name] = count.get(signal.name, 0) + 1
                ins.then_inc(signal, 1)
                pool.wait_ge(signal, count[signal.name])

            pool.dma_start(b2_sb[:, :, :].rearrange("p e d -> p (e d)"), b2r.partition_broadcast(P)).then_inc(ld_b2, 16)
            own(pool.memset(ident[:, :], 0.0))
            own(pool.memset(maskb[:, :, :], 0.0))
            own(pool.affine_select(out=ident[:, :], in_=ident[:, :], compare_op=ALU.not_equal, fill=1.0, base=0,
                                   pattern=[[-1, P]], channel_multiplier=1))
            own(pool.affine_select(out=maskb[:, :, :], in_=maskb[:, :, :], compare_op=ALU.is_ge, fill=SHUT, base=0,
                                   pattern=[[0, 4], [-1, P]], channel_multiplier=1))
            own(pool.tensor_copy(identb[:, :], ident[:, :]), consts)
            for b in range(KBUF):
                own(pool.memset(qx[64:P, b, :, :].bitcast(U32), 0), zeroed)
                own(pool.memset(kx[64:P, b, :, :].bitcast(U32), 0))
                own(pool.memset(kx[MROW:MROW + 2, b, :, :].bitcast(U32), ONES2), zeroed)
            pool.wait_ge(ld_x, 16)
            pool.wait_ge(ld_rows, 16)
            own(pool.tensor_tensor(xb[:, :, :], x_sb[:, :, :],
                                   R(BO).unsqueeze(1).to_broadcast([P, TILES, D]), ALU.add), xb_ready)
            own(pool.memset(blank[:, :], 0.0))
            own(pool.memset(blank[:, D:D + 1].bitcast(I32), NOBODY), blank_ready)
            own(pool.memset(mhalf[:, :], -0.5))
            own(pool.memset(x2[:, :, D:XW], 0.0))
            own(pool.iota(x2[:, :, D].bitcast(I32), pattern=[[P, TILES]], base=0, channel_multiplier=1))
            own(pool.memset(onesb[:, :], 1.0))
            pool.wait_ge(ld_tab, 16)
            own(pool.tensor_copy(regionb[:, :], region[0:1, :]))
            own(pool.affine_select(out=before[:, :], in_=onesb[:, :], compare_op=ALU.is_gt, fill=0.0, base=0,
                                   pattern=[[1, P]], channel_multiplier=-1), consts)
            norms = 0
            for kind, b, u in order:
                if kind == "exp" and u == NU - 1 and b + KBUF < B:
                    filled(pool, "s", (kind, b, u))
                    own(pool.memset(qx[MROW:MROW + 2, b % KBUF, :, :].bitcast(U32), 0), zeroed)
                if kind in ("out", "cross"):
                    norms += 1
                    pool.wait_ge(var_ready, norms)
                    k = 0 if kind == "out" else 1
                    own(pool.tensor_tensor(rstd[:, k, :], var[:, k, :], mhalf[:, 0:NT], ALU.pow), rstd_ready)
                if kind == "rank":
                    if b == B - 1:
                        pool.wait_ge(blanked, 16 * (E + 1))
                    pool.wait_ge(ranked, b + 1)
                    for n in range(b * NT, (b + 1) * NT):
                        pool.indirect_dma_start(out=sorted_dram, out_offset=bass.IndirectOffsetOnAxis(ap=slot32[:, n:n + 1], axis=0),
                                                in_=x2[:, n, :], in_offset=None).then_inc(placed, 16)
            for i in range(FT + 1):
                if i < FT:
                    norms += 1
                    pool.wait_ge(var_ready, norms)
                    own(pool.tensor_tensor(rstd[:, i % 2, 0:1], var[:, i % 2, 0:1], mhalf[:, 0:1], ALU.pow), rstd_ready)
                if i:
                    pool.wait_ge(yo_ready, i)
                    pool.indirect_dma_start(out=out, out_offset=bass.IndirectOffsetOnAxis(
                        ap=xt[i - 1][:, D:D + 1].bitcast(I32), axis=0), in_=yo[i - 1], in_offset=None,
                        bounds_check=B * S - 1, oob_is_err=False).then_inc(done, 16)
            pool.wait_ge(done, 16 * FT)

        @block.scalar
        def _(act):
            act.wait_ge(ld_x0, 48)
            act.activation(bqs[:, :], cols_sb[:, BQ:BQ + 1], ACT.Copy, scale=float(DK) ** -0.5).then_inc(qk_ready, 1)
            act.wait_ge(qk_ready, 1)
            n_sc = 0
            for piece in order:
                kind, b, u = piece
                if kind == "proj":
                    qk, free = filled(act, "m", piece, 0)
                    if b >= 2:
                        act.wait_ge(parts_ready, 2 * b - 2)
                    act.activation(qk32[:, b % 2, 0, :], qk[:, 0:S], ACT.Identity, bias=bqs[:, :],
                                   scale=float(DK) ** -0.5)
                    act.activation(qk32[:, b % 2, 1, :], qk[:, S:2 * S], ACT.Identity,
                                   bias=cols_sb[:, BK:BK + 1]).then_inc(free, 1)
                    taken(act, "m", piece, 0)
                    if b >= 2:
                        act.wait_ge(stored[b - 2], 16 * (1 + PARTS))
                    act.activation(parts[:, b % 2, 0, :, :], qk32[:, b % 2, :, :], ACT.Copy).then_inc(first_part, 1)
                    vp, free = filled(act, "m", piece, 1)
                    if b == 0:
                        act.wait_ge(vx_ready, 1)
                    if b >= KBUF:
                        act.wait_ge(pv_done, 4 * (b - KBUF + 1))
                    act.activation(vx[:, b % KBUF, :, :, 0:DK].rearrange("p t h d -> p (t h) d"),
                                   vp[:, 0:NT * D].rearrange("p (t h d) -> p (t h) d", t=NT, h=H), ACT.Copy).then_inc(free, 1)
                if kind == "ctx":
                    k2, free = filled(act, "m", piece, 0)
                    if b >= KBUF:
                        filled(act, "s", ("relu", b - KBUF, 0))
                    act.activation(k2T[:, b % KBUF, :], k2[:, :], ACT.Identity, bias=cols_sb[:, XBK:XBK + 1]).then_inc(free, 1)
                if kind == "shift":
                    mt, _f = filled(act, "m", piece)
                    if b >= 2:
                        act.wait_ge(shifted[b - 2], 32)
                    act.activation(mshift[:, b % 2, 0, :], mt[0:2 * H, 0:P], ACT.Copy, scale=-1.0).then_inc(mhi_ready, 1)
                if kind == "exp":
                    sc, free = filled(act, "s", piece)
                    k = NU * b + u
                    if k >= EBUF:
                        ob, ou = divmod(k - EBUF, NU)
                        act.wait_ge(pv_done, 4 * ob + (2 if ou < 3 else 4))
                    act.activation(es[:, k % EBUF, :], sc[:, :], ACT.Exp).then_inc(free, 1)
                if kind == "evac":
                    act.wait_ge(pv_done, 4 * b + 4)
                    if b:
                        act.wait_ge(turned, b)
                    act.activation(osb[:, 0:2, :], ps_o[:, 0:512].rearrange("p (g q) -> p g q", g=2), ACT.Copy)
                    act.activation(osb[:, 2:4, :], ps_o[:, 512:1024].rearrange("p (g q) -> p g q", g=2),
                                   ACT.Copy).then_inc(osb_ready, 1)
                if kind == "back":
                    at, free = filled(act, "m", piece)
                    act.activation(attnT[:, :], at[:, 0:S], ACT.Identity, bias=cols_sb[:, BV:BV + 1]).then_inc(free, 1)
                if kind == "x1t":
                    at, free = filled(act, "m", piece)
                    act.activation(x1T[:, :], at[:, 0:S], ACT.Copy).then_inc(free, 1)
                if kind == "q2":
                    at, free = filled(act, "m", piece)
                    act.activation(q2T[:, :], at[:, 0:S], ACT.Identity, bias=cols_sb[:, XBQ:XBQ + 1]).then_inc(free, 1)
                if kind == "relu":
                    at, free = filled(act, "s", piece)
                    act.activation(sc2[:, :, :], at[:, :].rearrange("p (k q) -> p k q", k=KT), ACT.Relu).then_inc(free, 1)
                if kind == "x2t":
                    at, free = filled(act, "m", piece)
                    act.activation(x2T[:, :], at[:, 0:S], ACT.Copy).then_inc(free, 1)
            act.wait_ge(ld_ffn, 32)
            act.wait_ge(table_ready, 2)
            for piece in tiles:
                kind, i, _u = piece
                if kind == "gather":
                    at, free = filled(act, "m", piece)
                    if i >= 2:
                        filled(act, "s", ("up", i - 2, 0))
                    act.activation(xsT[i % 2], at[:, 0:P], ACT.Copy).then_inc(free, 1)
                if kind == "up":
                    e = act.value_load(texp32[0:1, i:i + 1], min_val=0, max_val=E - 1)
                    at, free = filled(act, "s", piece)
                    if i >= 2:
                        filled(act, "m", ("down", i - 2, 0))
                    for c in range(FC):
                        ins = act.activation(hT[i % 2][:, c * P:(c + 1) * P], at[:, c * P:(c + 1) * P], ACT.Relu,
                                             bias=b1_sb[:, bass.ds(e * FC + c, 1)])
                    ins.then_inc(free, 1)

        @block.tensor
        def _(pe):
            pe.wait_ge(ld_x0, 48)
            for piece in order:
                kind, b, u = piece
                if kind == "proj":
                    if b == 1:
                        pe.wait_ge(ld_xT, 16)
                    xTb = xT_sb[:, b * S:(b + 1) * S]
                    qk, full = vacant(pe, "m", piece, 0)
                    pe.matmul(qk[:, 0:S], W(WQ), xTb, start=True, stop=True)
                    pe.matmul(qk[:, S:2 * S], W(WK), xTb, start=True, stop=True).then_inc(full, 1)
                    v, full = vacant(pe, "m", piece, 1)
                    for t in range(NT):
                        mm = pe.matmul(v[:, t * D:(t + 1) * D], xTb[:, t * P:(t + 1) * P], W(WV), start=True, stop=True)
                    mm.then_inc(full, 1)
                if kind == "ctx":
                    if b == 0:
                        pe.wait_ge(ld_ctx, 16)
                        pe.wait_ge(ld_w, 16)
                    cT = ctxT_sb[:, b * SK:(b + 1) * SK]
                    k2, full = vacant(pe, "m", piece, 0)
                    pe.matmul(k2[:, :], W(XK), cT, start=True, stop=True).then_inc(full, 1)
                    v, full = vacant(pe, "m", piece, 1)
                    for t in range(KT):
                        mm = pe.matmul(v[:, t * D:(t + 1) * D], cT[:, t * P:(t + 1) * P], W(XV), start=True, stop=True)
                    mm.then_inc(full, 1)
                if kind == "max":
                    if u == 0:
                        pe.wait_ge(spread[b], 16 * 2 * PARTS)
                        pe.wait_ge(zeroed, min(2 * b + 2, B + KBUF))
                        if b == 0:
                            pe.wait_ge(consts, 1)
                    sc, full = vacant(pe, "s", piece)
                    t, h0, _n = max_unit(u)
                    keys = (t + 1) * P
                    hs = 512 // keys
                    for bank in range(2):
                        o = sc[:, bank * 512:(bank + 1) * 512].rearrange("p (h k) -> p h k", h=hs)
                        pe.matmul(o[:, :, t * P:keys], identb[:, :], maskb[:, 0:hs, :], start=True, stop=False,
                                  skip_group_check=True)
                        for j in range(hs):
                            h = h0 + bank * hs + j
                            mm = pe.matmul(o[:, j, :], qx[:, b % KBUF, h, t * P:(t + 1) * P], kx[:, b % KBUF, h, 0:keys],
                                           start=False, stop=(j == hs - 1), skip_group_check=True)
                    mm.then_inc(full, 1)
                if kind == "shift":
                    for last in (NU - 2, NU - 1):
                        taken(pe, "s", ("max", b, last))
                    mt, full = vacant(pe, "m", piece)
                    pe.transpose(mt[0:2 * H, 0:P], mx[:, b % 2, :, :].rearrange("p h t -> p (h t)"),
                                 ident[:, :]).then_inc(full, 1)
                if kind == "exp":
                    if u == 0:
                        pe.wait_ge(shifted[b], 32)
                    sc, full = vacant(pe, "s", piece)
                    kt, h0, n = UNITS[u]
                    qs = S - kt * P
                    for j in range(n):
                        h = h0 + j
                        mm = pe.matmul(sc[:, j * qs:(j + 1) * qs], kx[:, b % KBUF, h, kt * P:(kt + 1) * P],
                                       qx[:, b % KBUF, h, kt * P:S], start=True, stop=True)
                    mm.then_inc(full, 1)
                if kind == "pv":
                    pe.wait_ge(p_ready, NU * b + (3 if u < 2 else 6))
                    if u == 0:
                        taken(pe, "m", ("proj", b, 0), 1)
                        if b:
                            pe.wait_ge(attn_ready, b)
                    for kt in range(NT):
                        for j in range(4):
                            h = 4 * u + j
                            k, at = where(kt, h)
                            qs = S - kt * P
                            mm = pe.matmul(ps_o[VW * j:VW * (j + 1), u * S + kt * P:(u + 1) * S], vx[:, b % KBUF, kt, h, :],
                                           es[:, (NU * b + k) % EBUF, at:at + qs], start=(kt == 0), stop=(kt == 1))
                    mm.then_inc(pv_done, 1)
                if kind == "turn":
                    pe.wait_ge(osb_ready, b + 1)
                    for t in range(NT):
                        for g in range(4):
                            mm = pe.transpose(ps_o[:, t * 512 + g * P:t * 512 + (g + 1) * P],
                                              osb[:, g, t * P:(t + 1) * P], ident[:, :])
                    mm.then_inc(turned, 1)
                if kind == "back":
                    pe.wait_ge(attn_ready, b + 1)
                    at, full = vacant(pe, "m", piece)
                    for t in range(NT):
                        mm = pe.transpose(at[:, t * P:(t + 1) * P], attn[:, t, :], ident[:, :])
                    mm.then_inc(full, 1)
                if kind == "out":
                    taken(pe, "m", ("back", b, 0))
                    y, full = vacant(pe, "m", piece)
                    for t in range(NT):
                        mm = pe.matmul(y[:, t * D:(t + 1) * D], attnT[:, t * P:(t + 1) * P], W(WO), start=True, stop=True)
                    mm.then_inc(full, 1)
                if kind == "x1t":
                    pe.wait_ge(x1_ready, b + 1)
                    at, full = vacant(pe, "m", piece)
                    for t in range(NT):
                        mm = pe.transpose(at[:, t * P:(t + 1) * P], x1[:, b * NT + t, :], ident[:, :])
                    mm.then_inc(full, 1)
                if kind == "q2":
                    taken(pe, "m", ("x1t", b, 0))
                    at, full = vacant(pe, "m", piece)
                    pe.matmul(at[:, 0:S], W(XQ), x1T[:, :], start=True, stop=True).then_inc(full, 1)
                if kind == "relu":
                    taken(pe, "m", ("q2", b, 0))
                    taken(pe, "m", ("ctx", b, 0))
                    at, full = vacant(pe, "s", piece)
                    for k in range(KT):
                        mm = pe.matmul(at[:, k * S:(k + 1) * S], k2T[:, b % KBUF, k * P:(k + 1) * P], q2T[:, :],
                                       start=True, stop=True)
                    mm.then_inc(full, 1)
                if kind == "cross":
                    taken(pe, "s", ("relu", b, 0))
                    taken(pe, "m", ("ctx", b, 0), 1)
                    at, full = vacant(pe, "m", piece)
                    for t in range(NT):
                        for k in range(KT):
                            mm = pe.matmul(at[:, t * D:(t + 1) * D], sc2[:, k, t * P:(t + 1) * P], v2[:, b % KBUF, k, :],
                                           start=(k == 0), stop=(k == KT - 1))
                    mm.then_inc(full, 1)
                if kind == "x2t":
                    pe.wait_ge(x2_ready, b + 1)
                    at, full = vacant(pe, "m", piece)
                    for t in range(NT):
                        mm = pe.transpose(at[:, t * P:(t + 1) * P], x2[:, b * NT + t, 0:D], ident[:, :])
                    mm.then_inc(full, 1)
                if kind == "route":
                    taken(pe, "m", ("x2t", b, 0))
                    at, full = vacant(pe, "m", piece)
                    for t in range(NT):
                        mm = pe.matmul(at[:, t * E:(t + 1) * E], x2T[:, t * P:(t + 1) * P], W(WR),
                                       start=True, stop=True)
                    mm.then_inc(full, 1)
                if kind == "rank":
                    pe.wait_ge(hot_ready, b + 1)
                    if b == 0:
                        pe.wait_ge(consts, 2)
                    at, full = vacant(pe, "m", piece)
                    for t in range(NT + 1):
                        n = b * NT + t
                        o = at[:, t * E:(t + 1) * E]
                        if t < NT:
                            pe.matmul(o, onesb[0:1, :], regionb[0:1, :], start=True, stop=False)
                            pe.matmul(o, before[:, :], hotb[:, n, :], start=False, stop=(n == 0))
                        for m in range(n):
                            mm = pe.matmul(o, onesb[:, :], hotb[:, m, :], start=(m == 0 and t == NT), stop=(m == n - 1))
                    mm.then_inc(full, 1)
            pe.wait_ge(ld_ffn, 32)
            for piece in tiles:
                kind, i, _u = piece
                if kind == "gather":
                    pe.wait_ge(xt_full[i], 16)
                    at, full = vacant(pe, "m", piece)
                    pe.transpose(at[:, 0:P], xt[i][:, 0:D], ident[:, :]).then_inc(full, 1)
                if kind == "up":
                    pe.wait_ge(w1_full[i % WBUF], 16 * (i // WBUF + 1))
                    taken(pe, "m", ("gather", i, 0))
                    at, full = vacant(pe, "s", piece)
                    for c in range(FC):
                        mm = pe.matmul(at[:, c * P:(c + 1) * P], w1_t[i % WBUF][:, c * P:(c + 1) * P], xsT[i % 2],
                                       start=True, stop=True)
                    mm.then_inc(full, 1)
                if kind == "down":
                    expert = pe.value_load(texp32[0:1, i:i + 1], min_val=0, max_val=E - 1)
                    taken(pe, "s", ("up", i, 0))
                    at, full = vacant(pe, "m", piece)
                    for c in range(FC):
                        mm = pe.matmul(at[:, 0:D], hT[i % 2][:, c * P:(c + 1) * P], w2_sb[:, bass.ds(expert, 1), c, :].rearrange("p a d -> p (a d)"),
                                       start=(c == 0), stop=(c == FC - 1))
                    mm.then_inc(full, 1)

        @block.vector
        def _(v):
            link = [0]

            def own(ins):
                link[0] += 1
                ins.then_inc(dve, 1)
                v.wait_ge(dve, link[0])

            norms = [0]

            def variance(k):
                for t in range(NT):
                    ins = v.bn_stats(stats[:, t, :], z[k][:, t, :])
                own(ins)
                for t in range(NT):
                    ins = v.bn_aggr(mv[:, k, t, :], stats[:, t, :])
                own(ins)
                norms[0] += 1
                v.tensor_scalar(var[:, k, :], mv[:, k, :, 1], EPS, None, ALU.add).then_inc(var_ready, 1)

            def normalise(k, dst, ready):
                for t in range(NT):
                    ins = v.tensor_scalar(dst[:, t, :], z[k][:, t, :], mv[:, k, t, 0:1], rstd[:, k, t:t + 1],
                                          ALU.subtract, ALU.mult)
                ins.then_inc(ready, 1)

            v.memset(vx[:, :, :, :, :].rearrange("p b t h w -> p (b t h) w")[:, :, DK + 1:VW], 0.0)
            v.memset(vx[:, :, :, :, :].rearrange("p b t h w -> p (b t h) w")[:, :, DK:DK + 1], 1.0)\
                .then_inc(vx_ready, 1)
            v.wait_ge(ld_tab, 16)
            for piece in order:
                kind, b, u = piece
                if kind == "proj":
                    v.wait_ge(first_part, b + 1)
                    qk, r = qk32[:, b % 2, :, :], rest[:, b % 2, :, :]
                    p = [parts[:, b % 2, i, :, :] for i in range(PARTS)]
                    own(v.tensor_tensor(r, qk, p[0], ALU.subtract))
                    own(v.tensor_copy(p[1], r))
                    v.tensor_tensor(p[2], r, p[1], ALU.subtract).then_inc(parts_ready, 1)
                    v.tensor_copy(parts[:, b % 2, PARTS:2 * PARTS - 1, 1, :], parts[:, b % 2, 0:PARTS - 1, 1, :])\
                        .then_inc(parts_ready, 1)
                if kind == "ctx":
                    vp, free = filled(v, "m", piece, 1)
                    v.wait_ge(ld_rows, 16)
                    if b >= KBUF:
                        filled(v, "m", ("cross", b - KBUF, 0))
                    v.tensor_tensor(v2[:, b % KBUF, :, :], vp[:, :].rearrange("p (k d) -> p k d", k=KT),
                                    R(XBV).unsqueeze(1).to_broadcast([P, KT, D]), ALU.add).then_inc(free, 1)
                if kind == "max":
                    sc, free = filled(v, "s", piece)
                    t, h0, n = max_unit(u)
                    keys = (t + 1) * P
                    if u == 0 and b >= 2:
                        filled(v, "m", ("shift", b - 2, 0))
                    v.tensor_reduce(mx[:, b % 2, h0:h0 + n, t], sc[:, :].rearrange("p (h k) -> p h k", h=n), AX.X,
                                    ALU.max).then_inc(free, 1)
                if kind == "shift":
                    mt, free = filled(v, "m", piece)
                    v.wait_ge(mhi_ready, b + 1)
                    v.scalar_tensor_tensor(out=mshift[:, b % 2, 1, :], in0=mt[0:2 * H, 0:P], scalar=-1.0,
                                           in1=mshift[:, b % 2, 0, :], op0=ALU.mult, op1=ALU.subtract).then_inc(free, 1)
                if kind == "exp":
                    taken(v, "s", piece)
                    kt, h0, nh = UNITS[u]
                    qs = S - kt * P
                    e = es[:, (NU * b + u) % EBUF, :].rearrange("p (h q) -> p h q", h=nh)
                    v.scalar_tensor_tensor(out=e, in0=e, scalar=CEIL, in1=decay[:, 0:qs].unsqueeze(1).to_broadcast([P, nh, qs]),
                                           op0=ALU.min, op1=ALU.mult).then_inc(p_ready, 1)
                if kind == "turn":
                    v.wait_ge(turned, b + 1)
                    o = ps_o[:, :].rearrange("p (t h w) -> p t h w", t=NT, h=H)
                    if b:
                        filled(v, "m", ("back", b - 1, 0))
                    for t in range(NT):
                        ins = v.reciprocal(rden[:, t, :], o[:, t, :, DK])
                    own(ins)
                    for t in range(NT):
                        ins = v.tensor_tensor(attn[:, t, :].rearrange("p (h d) -> p h d", h=H), o[:, t, :, 0:DK],
                                              rden[:, t, :].unsqueeze(2).to_broadcast([P, H, DK]), ALU.mult)
                        if t == 0:
                            own(ins)
                    ins.then_inc(attn_ready, 1)
                if kind == "out":
                    y, free = filled(v, "m", piece)
                    v.wait_ge(xb_ready, 1)
                    if b:
                        v.wait_ge(x1_ready, b)
                    ins = v.tensor_tensor(z[0][:, :, :], y[:, 0:NT * D].rearrange("p (t d) -> p t d", t=NT),
                                          xb[:, b * NT:(b + 1) * NT, :], ALU.add)
                    ins.then_inc(free, 1)
                    taken(v, "m", piece)
                    variance(0)
                if kind == "norm1":
                    v.wait_ge(rstd_ready, norm_at[("out", b, 0)])
                    normalise(0, x1[:, b * NT:(b + 1) * NT, :], x1_ready)
                if kind == "cross":
                    y, free = filled(v, "m", piece)
                    v.wait_ge(x1_ready, b + 1)
                    if b:
                        v.wait_ge(x2_ready, b)
                    ins = v.tensor_tensor(z[1][:, :, :], y[:, 0:NT * D].rearrange("p (t d) -> p t d", t=NT),
                                          x1[:, b * NT:(b + 1) * NT, :], ALU.add)
                    ins.then_inc(free, 1)
                    taken(v, "m", piece)
                    variance(1)
                if kind == "norm2":
                    v.wait_ge(rstd_ready, norm_at[("cross", b, 0)])
                    normalise(1, x2[:, b * NT:(b + 1) * NT, 0:D], x2_ready)
                if kind == "route":
                    at, free = filled(v, "m", piece)
                    hb = hot[:, :, :]
                    if b:
                        v.wait_ge(hot_ready, b)
                    v.tensor_tensor(lg[:, :, :], at[:, 0:NT * E].rearrange("p (t e) -> p t e", t=NT),
                                    R(BR).unsqueeze(1).to_broadcast([P, NT, E]), ALU.add).then_inc(free, 1)
                    taken(v, "m", piece)
                    own(v.tensor_reduce(lgmax[:, :], lg[:, :, :], AX.X, ALU.max))
                    own(v.tensor_tensor(hb, lg[:, :, :], lgmax[:, :].unsqueeze(2).to_broadcast([P, NT, E]), ALU.is_ge))
                    own(v.tensor_tensor(lg[:, :, :], hb, rank8[:, :].unsqueeze(1).to_broadcast([P, NT, E]), ALU.mult))
                    own(v.tensor_reduce(lgmax[:, :], lg[:, :, :], AX.X, ALU.max))
                    v.tensor_tensor(hotb[:, b * NT:(b + 1) * NT, :], lg[:, :, :],
                                    lgmax[:, :].unsqueeze(2).to_broadcast([P, NT, E]), ALU.is_equal).then_inc(hot_ready, 1)
                if kind == "rank":
                    at, free = filled(v, "m", piece)
                    own(v.tensor_tensor(lg[:, :, :], at[:, 0:NT * E].rearrange("p (t e) -> p t e", t=NT),
                                        hotb[:, b * NT:(b + 1) * NT, :], ALU.mult))
                    own(v.tensor_reduce(slotf[:, :], lg[:, :, :], AX.X, ALU.add))
                    v.tensor_copy(slot32[:, b * NT:(b + 1) * NT], slotf[:, :]).then_inc(ranked, 1)
                    if b == B - 2:
                        v.tensor_tensor(end32[:, :], at[0:1, NT * E:(NT + 1) * E], region[0:1, :], ALU.add).then_inc(ends_ready, 1)
                    v.tensor_copy(total[:, :], at[0:1, NT * E:(NT + 1) * E]).then_inc(free, 1)
            taken(v, "m", ("rank", B - 1, 0))
            own(v.tensor_tensor(more[:, :, :], total[:, :].unsqueeze(2).to_broadcast([1, E, E]),
                                fills.unsqueeze(1).to_broadcast([1, E, E]), ALU.is_gt))
            own(v.tensor_reduce(ntile[:, :], more[:, :, :], AX.X, ALU.add))
            own(v.tensor_tensor(more[:, :, :], lower, ntile[:, :].unsqueeze(1).to_broadcast([1, E, E]), ALU.mult))
            own(v.tensor_reduce(ends[:, :], more[:, :, :], AX.X, ALU.add))
            own(v.tensor_tensor(past[:, :, :], ends[:, :].unsqueeze(1).to_broadcast([1, FTP, E]), number, ALU.is_le))
            own(v.tensor_reduce(texp[:, :], past[:, :, :], AX.X, ALU.add))
            own(v.tensor_tensor(past2[:, :, :], past[:, :, :], ntile[:, :].unsqueeze(1).to_broadcast([1, FTP, E]), ALU.mult))
            own(v.tensor_reduce(tfirst[:, :], past2[:, :, :], AX.X, ALU.add))
            v.tensor_scalar(texp32[:, :], texp[:, :], E - 1.0, None, ALU.min).then_inc(table_ready, 1)
            own(v.scalar_tensor_tensor(out=tfirst[:, :], in0=texp[:, :], scalar=float(REGION // P), in1=tfirst[:, :],
                                       op0=ALU.mult, op1=ALU.subtract))
            own(v.tensor_tensor(tfirst[:, :], tfirst[:, :], number[:, :, 0], ALU.add))
            v.tensor_scalar(trow32[:, :], tfirst[:, :], float(P), float(E * REGION), ALU.mult, ALU.min).then_inc(table_ready, 1)
            v.wait_ge(table_ready, 2)
            v.wait_ge(ld_b2, 16)

            def residual(i):
                e = v.value_load(texp32[0:1, i:i + 1], min_val=0, max_val=E - 1)
                v.wait_ge(xt_full[i], 16)
                return v.tensor_tensor(xres[i % 2], xt[i][:, 0:D],
                                       b2_sb[:, bass.ds(e, 1), :].rearrange("p a d -> p (a d)"), ALU.add)

            def normalise_tile(i, norm):
                k = i % 2
                v.wait_ge(rstd_ready, norm)
                v.tensor_scalar(yo[i], zt[k], mv[:, k, 0, 0:1], rstd[:, k, 0:1], ALU.subtract, ALU.mult).then_inc(yo_ready, 1)

            own(residual(0))
            for piece in tiles:
                kind, i, _u = piece
                if kind == "down":
                    at, free = filled(v, "m", piece)
                    k = i % 2
                    v.tensor_tensor(zt[k], at[:, 0:D], xres[k], ALU.add).then_inc(free, 1)
                    if i:
                        normalise_tile(i - 1, norms[0])
                    taken(v, "m", piece)
                    own(v.bn_stats(st[k], zt[k]))
                    v.bn_aggr(mv[:, k, 0, :], st[k]).then_inc(dve, 1)
                    link[0] += 1
                    if i + 1 < FT:
                        own(residual(i + 1))
                    else:
                        v.wait_ge(dve, link[0])
                    norms[0] += 1
                    v.tensor_scalar(var[:, k, 0:1], mv[:, k, 0, 1:2], EPS, None, ALU.add).then_inc(var_ready, 1)
            normalise_tile(FT - 1, norms[0])


NTAB = S + 3 * E + E * E + FTP * E


def shape_tables(np):
    late = np.arange(S)[None, :] - np.arange(P)[:, None]
    decay = np.where(late >= 0, np.maximum(late, 1).astype(np.float64) ** -DECAY, 0.0)
    e = np.arange(E)
    flat = [E - e, REGION * e, P * e, (e[None, :] <= e[:, None]).ravel(), np.repeat(np.arange(FTP), E)]
    flat = np.concatenate(flat)
    return np.concatenate([decay, np.broadcast_to(flat, (P, flat.size))], axis=1).astype(np.float32)


def max_unit(u):
    return (0, 8 * u, 8) if u < 2 else (1, 4 * (u - 2), 4)


def where(kt, h):
    for k, (t, h0, n) in enumerate(UNITS):
        if t == kt and h0 <= h < h0 + n:
            return k, (h - h0) * (S - kt * P)


def kernel(**inputs):
    import numpy as np
    import concourse.bacc as bacc
    from concourse.bass_utils import run_bass_kernel_spmd as run

    a = {k: np.asarray(v) for k, v in inputs.items()}
    arrays = {
        "xtok": a["x"].reshape(B * S, D),
        "xT": a["x"].reshape(B * S, D).T,
        "ctxT": a["ctx_1024"].reshape(B * SK, D).T,
        "wts": np.concatenate([a["L0_attn_Wq"], a["L0_attn_Wk"], a["L0_attn_Wv"], a["L0_attn_Wo"], a["L0_xattn_Wq"].T,
                               a["L0_xattn_Wk"].T, a["L0_xattn_Wv"].T, a["L0_ffn_Wr"].T], axis=1),
        "cols": np.stack([a["L0_attn_bq"], a["L0_attn_bk"], a["L0_xattn_bq"], a["L0_xattn_bk"], a["L0_attn_bv"]], axis=1),
        "rows": np.concatenate([a["L0_attn_bo"], a["L0_xattn_bv"], a["L0_ffn_br"]]),
        "w1T": a["L0_ffn_W1"].transpose(2, 0, 1).reshape(D, E * FF),
        "w2T": a["L0_ffn_W2"].reshape(E, D, FC, P).transpose(3, 0, 2, 1).reshape(P, E * FC * D),
        "b1c": a["L0_ffn_b1"].reshape(E, FC, P).transpose(2, 0, 1).reshape(P, E * FC),
        "b2r": a["L0_ffn_b2"].reshape(E * D),
        "tables": shape_tables(np),
    }
    nc = bacc.Bacc("TRN2", target_bir_lowering=False, num_devices=1)
    args = []
    for name, v in arrays.items():
        arrays[name] = np.ascontiguousarray(v)
        args.append(nc.dram_tensor(name, v.shape, mybir.dt.from_np(v.dtype), kind="ExternalInput").ap())
    args.append(nc.dram_tensor("out", (B * S, D), F32, kind="ExternalOutput").ap())
    decoder_kernel(nc, *args)
    r = run(nc, [arrays], core_ids=[0])
    return r.results[0]["out"].reshape(B, S, D)
```

```python
from contextlib import ExitStack

import concourse.bass as bass
from concourse import mybir

F32 = mybir.dt.float32
BF16 = mybir.dt.bfloat16
I32 = mybir.dt.int32
U32 = mybir.dt.uint32
ALU = mybir.AluOpType
ACT = mybir.ActivationFunctionType
AX = mybir.AxisListType

P = 128
B, S, D = 4, 256, 128
NT = S // P
TILES = B * NT
H = 16
DK = D // H
SK = 512
KT = SK // P
E, FF = 8, 512
FC = FF // P
PARTS = 3
MROW = 96
VW = 32
EPS = 1e-5
DECAY = 0.25
REGION = B * S + P
ROWS = E * REGION + P
LATE = S // P + 1
XW = D + 4
NOBODY = 1 << 20
FT = (B * S - E) // P + E
FT_OFTEN = FT - 2
EBITS, EWORD = 3, 8
RBITS, RWORD = 7, 3
FTE = -(-FT // EWORD) * EWORD
FTR = -(-FT // RWORD) * RWORD
FTP = max(FTE, FTR)
assert E <= 1 << EBITS and ROWS // P <= 1 << RBITS
WBUF = 6
ONES2 = 0x3F803F80
SHUT = -1e30
CEIL = 1e30

UNITS = [(0, 0, 4), (0, 4, 4), (1, 0, 8), (0, 8, 4), (0, 12, 4), (1, 8, 8)]
NU = len(UNITS)
KBUF = 3
EBUF = 7


START = [("proj", 0, 0), ("proj", 1, 0), ("ctx", 0, 0), ("ctx", 1, 0), ("max", 0, 0), ("max", 0, 1),
         ("max", 0, 2), ("max", 0, 3), ("max", 0, 4), ("max", 0, 5), ("shift", 0, 0), ("shift", 0, 1)]
ROUND = [("pv", -1, 2), ("max", 1, 0), ("pv", -1, 3), ("evac", -1, 0), ("max", 1, 1), ("x2t", -2, 0),
         ("max", 1, 2), ("turn", -1, 0), ("exp", 0, 0), ("exp", 0, 1), ("back", -1, 0), ("out", -1, 0),
         ("exp", 0, 2), ("norm1", -1, 0), ("proj", 2, 0), ("route", -2, 0), ("exp", 0, 3), ("exp", 0, 4),
         ("x1t", -1, 0), ("exp", 0, 5), ("max", 1, 3), ("q2", -1, 0), ("pv", 0, 0), ("relu", -1, 0),
         ("pv", 0, 1), ("rank", -2, 0), ("shift", 1, 0), ("max", 1, 4), ("max", 1, 5), ("cross", -1, 0),
         ("ctx", 2, 0), ("shift", 1, 1), ("norm2", -1, 0)]
CHAIN = [("pv", -1, 2), ("pv", -1, 3), ("evac", -1, 0), ("turn", -1, 0), ("back", -1, 0), ("out", -1, 0),
         ("x2t", -2, 0), ("warm", -1, 8), ("norm1", -1, 0), ("route", -2, 0), ("x1t", -1, 0),
         ("warm", -1, 2), ("q2", -1, 0), ("rank", -2, 0), ("warm", -1, 1), ("relu", -1, 0), ("cross", -1, 0),
         ("warm", -1, 6), ("norm2", -1, 0), ("x2t", -1, 0), ("warm", -1, 2), ("route", -1, 0),
         ("rank", -1, 0), ("warm", -1, 18)]


def schedule():
    out = list(START)
    for r in range(B):
        out += [(kind, r + rel, u) for kind, rel, u in ROUND if 0 <= r + rel < B and (r > 0 or rel >= 0)]
    return out + [(kind, B + rel, u) for kind, rel, u in CHAIN]


def expert_schedule(first, past):
    out = [("gather", first, 0)]
    for i in range(first, past + 1):
        out += [("gather", i + 1, 0), ("up", i, 0), ("down", i - 1, 0)]
    return [p for p in out if first <= p[1] < past]


USES = {"proj": "mm", "ctx": "mm", "max": "s", "shift": "m", "exp": "s", "back": "m", "out": "m",
        "x1t": "m", "q2": "m", "relu": "s", "cross": "m", "x2t": "m", "route": "m", "rank": "m",
        "gather": "m", "up": "s", "down": "m"}


def slots(order):
    at = {"s": 0, "m": 0}
    out = {}
    for piece in order:
        for j, ring in enumerate(USES.get(piece[0], "")):
            out[(*piece, j)] = (at[ring] % 2, at[ring] // 2)
            at[ring] += 1
    return out


def decoder_kernel(nc, xtok, xT, ctxT, wts, cols, rows, w1T, w2T, b1c, b2r, tables, out):
    order = schedule()
    spans = [(0, FT_OFTEN), (FT_OFTEN, FT)]
    place = slots(order + expert_schedule(*spans[0]) + expert_schedule(*spans[1]))
    norm_at = {p: n + 1 for n, p in enumerate(q for q in order if q[0] in ("out", "cross"))}
    norms = len(norm_at)
    WQ, WK, WV, WO, XQ, XK, XV, WR = range(8)
    BQ, BK, XBQ, XBK, BV = range(5)
    BO, XBV, BR = range(3)
    parts_dram = nc.dram_tensor("parts_dram", [B, 1 + PARTS, D, PARTS * S], BF16, kind="Internal").ap()
    sorted_dram = nc.dram_tensor("sorted_dram", [ROWS, XW], F32, kind="Internal").ap()

    with ExitStack() as ctx:
        def sb(name, shape, dt=F32):
            return ctx.enter_context(nc.sbuf_tensor(name, shape, dt))

        def psum(name, cols_):
            return ctx.enter_context(nc.psum_tensor(name, [P, cols_], F32))

        def sem(name):
            return ctx.enter_context(nc.semaphore(name))

        w_sb = sb("w_sb", [P, 7 * D + E])
        cols_sb = sb("cols_sb", [P, 5])
        rows_sb = sb("rows_sb", [P, 2 * D + E])
        xT_sb = sb("xT_sb", [P, B * S])
        x_sb = sb("x_sb", [P, TILES, D])
        ctxT_sb = sb("ctxT_sb", [P, B * SK])
        w2_sb = sb("w2_sb", [P, E, FC, D])
        b1_sb = sb("b1_sb", [P, E * FC])
        b2_sb = sb("b2_sb", [P, E, D])
        tab_sb = sb("tab_sb", [P, NTAB])

        def W(i):
            return w_sb[:, i * D:(i + 1) * D] if i < WR else w_sb[:, WR * D:WR * D + E]

        def R(i):
            return rows_sb[:, i * D:(i + 1) * D] if i < BR else rows_sb[:, BR * D:BR * D + E]

        ident = sb("ident", [P, P])
        identb = sb("identb", [P, P], BF16)
        maskb = sb("maskb", [P, 4, P], BF16)
        before = sb("before", [P, P], BF16)
        onesb = sb("onesb", [P, P], BF16)
        blank = sb("blank", [P, XW])
        mhalf = sb("mhalf", [P, NT])
        bq_scaled = sb("bq_scaled", [P, 1])

        decay = tab_sb[:, 0:S]
        rank8 = tab_sb[:, S:S + E]
        region = tab_sb[:, S + E:S + 2 * E]
        fills = tab_sb[0:1, S + 2 * E:S + 3 * E]
        lower = tab_sb[0:1, S + 3 * E:S + 3 * E + E * E].rearrange("p (a b) -> p a b", a=E)
        number = tab_sb[0:1, S + 3 * E + E * E:S + 3 * E + E * E + FTP * E].rearrange("p (i e) -> p i e", e=E)
        eplace = tab_sb[0:1, NTAB - 2 * FTP:NTAB - FTP]
        rplace = tab_sb[0:1, NTAB - FTP:NTAB]

        qk32 = sb("qk32", [P, 2, 2, S])
        rest = sb("rest", [P, 2, 2, S])
        parts = sb("parts", [P, 2, 2 * PARTS - 1, 2, S], BF16)
        qx = sb("qx", [P, KBUF, H, S], BF16)
        kx = sb("kx", [P, KBUF, H, S], BF16)
        vx = sb("vx", [P, KBUF, NT, H, VW])
        mx = sb("mx", [P, 2, H, NT])
        mshift = sb("mshift", [H, 2, 2, 2, P], BF16)
        es = sb("es", [P, EBUF, 1024])
        osb = sb("osb", [P, 4, S])
        rden = sb("rden", [P, NT, H])
        attn = sb("attn", [P, NT, D])
        attnT = sb("attnT", [P, S])
        z = [sb(f"z{k}", [P, NT, D]) for k in range(2)]
        stats = sb("stats", [P, NT, 6])
        mv = sb("mv", [P, 2, NT, 2])
        rstd = sb("rstd", [P, 2, NT])
        var = sb("var", [P, 2, NT])
        x1 = sb("x1", [P, TILES, D])
        x1T = sb("x1T", [P, S])
        q2T = sb("q2T", [P, S])
        k2T = sb("k2T", [P, KBUF, SK])
        v2 = sb("v2", [P, KBUF, KT, D])
        sc2 = sb("sc2", [P, KT, S])
        x2 = sb("x2", [P, TILES, XW])
        x2T = sb("x2T", [P, S])
        lg = sb("lg", [P, NT, E])
        lgmax = sb("lgmax", [P, NT])
        hot = sb("hot", [P, NT, E])
        hotb = sb("hotb", [P, TILES, E], BF16)
        slotf = sb("slotf", [P, NT])
        regionb = sb("regionb", [1, E], BF16)
        slot32 = sb("slot32", [P, TILES], I32)
        total = sb("total", [1, E])
        more = sb("more", [1, E, E])
        ntile = sb("ntile", [1, E])
        ends = sb("ends", [1, E])
        past = sb("past", [1, FTP, E])
        past2 = sb("past2", [1, FTP, E])
        texp = sb("texp", [1, FTP])
        tfirst = sb("tfirst", [1, FTP])
        end32 = sb("end32", [1, E], I32)
        ntiles32 = sb("ntiles32", [1, 1], I32)
        eword = sb("eword", [1, FTE // EWORD])
        rword = sb("rword", [1, FTR // RWORD])
        eword32 = sb("eword32", [1, FTE // EWORD], I32)
        rword32 = sb("rword32", [1, FTR // RWORD], I32)
        room = es[:, :, :].rearrange("p k n -> p (k n)")
        w1_t = [room[:, k * FF:(k + 1) * FF] for k in range(WBUF)]
        at = WBUF * FF
        hT = [room[:, at + k * FF:at + (k + 1) * FF] for k in range(2)]
        at += 2 * FF
        xsT = [room[:, at + k * P:at + (k + 1) * P] for k in range(2)]
        at += 2 * P
        zt = [room[:, at + k * D:at + (k + 1) * D] for k in range(2)]
        at += 2 * D
        xres = [room[:, at + k * D:at + (k + 1) * D] for k in range(2)]
        token_room = qx[:, :, :, :].rearrange("p b h t -> p (b h t)").bitcast(F32)
        xt = [token_room[:, i * XW:(i + 1) * XW] for i in range(FT)]
        yo = [token_room[:, FT * XW + i * D:FT * XW + (i + 1) * D] for i in range(FT)]
        st = [stats[:, k, :] for k in range(2)]

        ps_s = [psum(f"ps_s{i}", 1024) for i in range(2)]
        ps_m = [psum(f"ps_m{i}", 512) for i in range(2)]
        ps_o = psum("ps_o", 1024)

        s_full = [sem(f"s_full{i}") for i in range(2)]
        s_free = [sem(f"s_free{i}") for i in range(2)]
        m_full = [sem(f"m_full{i}") for i in range(2)]
        m_free = [sem(f"m_free{i}") for i in range(2)]
        ring = {"s": (ps_s, s_full, s_free), "m": (ps_m, m_full, m_free)}

        ld_w = sem("ld_w")
        ld_rows = sem("ld_rows")
        ld_x0 = sem("ld_x0")
        ld_xT = sem("ld_xT")
        ld_x = sem("ld_x")
        ld_ctx = [sem(f"ld_ctx{i}") for i in range(2)]
        ld_ffn = sem("ld_ffn")
        stored = [[sem(f"stored{b}_{k}") for k in range(1 + PARTS)] for b in range(B)]
        spread = [sem(f"spread{b}") for b in range(B)]
        shifted = [[sem(f"shifted{b}_{u}") for u in range(2)] for b in range(B)]
        pool_done = sem("pool_done")
        consts = sem("consts")
        zeroed = sem("zeroed")
        residual_ready = sem("residual_ready")
        dve = sem("dve")
        var_ready = sem("var_ready")
        rstd_ready = sem("rstd_ready")
        vx_ready = sem("vx_ready")
        first_part = sem("first_part")
        bq_ready = sem("bq_ready")
        parts_ready = sem("parts_ready")
        mhi_ready = sem("mhi_ready")
        p_ready = sem("p_ready")
        pv_done = sem("pv_done")
        osb_ready = sem("osb_ready")
        turned = sem("turned")
        attn_ready = sem("attn_ready")
        x1_ready = sem("x1_ready")
        x2_ready = sem("x2_ready")
        hot_ready = sem("hot_ready")
        ranked = sem("ranked")
        blanked = sem("blanked")
        blank_ready = sem("blank_ready")
        placed = sem("placed")
        table_ready = sem("table_ready")
        ld_b2 = sem("ld_b2")
        ld_tab = sem("ld_tab")
        xt_full = [sem(f"xt_full{i}") for i in range(FT)]
        w1_full = [sem(f"w1_full{i}") for i in range(WBUF)]
        ends_ready = sem("ends_ready")
        yo_ready = sem("yo_ready")
        done = sem("done")

        block = ctx.enter_context(nc.Block())

        def filled(eng, name, piece, j=0):
            slot, n = place[(*piece, j)]
            eng.wait_ge(ring[name][1][slot], n + 1)
            return ring[name][0][slot], ring[name][2][slot]

        def taken(eng, name, piece, j=0):
            slot, n = place[(*piece, j)]
            eng.wait_ge(ring[name][2][slot], n + 1)

        def vacant(pe, name, piece, j=0):
            slot, n = place[(*piece, j)]
            if n:
                pe.wait_ge(ring[name][2][slot], n)
            return ring[name][0][slot], ring[name][1][slot]

        def word_values(eng, words, k, bits, per_word, top):
            word = eng.value_load(words[0:1, k:k + 1], min_val=0, max_val=(1 << bits * per_word) - 1)
            return [((word >> bits * i) & ((1 << bits) - 1)).with_bounds(min_val=0, max_val=top)
                    for i in range(per_word)]

        def tile_experts(eng):
            return [e for k in range(FTE // EWORD) for e in word_values(eng, eword32, k, EBITS, EWORD, E - 1)]

        def tile_count(eng):
            return eng.value_load(ntiles32[0:1, 0:1], min_val=0, max_val=FT)

        @block.sync
        def _(sp):
            sp.dma_start(w_sb[:, 0:3 * D], wts[:, 0:3 * D]).then_inc(ld_x0, 16)
            sp.dma_start(xT_sb[:, 0:S], xT[:, 0:S]).then_inc(ld_x0, 16)
            sp.dma_start(cols_sb[:, :], cols).then_inc(ld_x0, 16)
            sp.dma_start(xT_sb[:, S:], xT[:, S:]).then_inc(ld_xT, 16)
            sp.dma_start(w_sb[:, 3 * D:], wts[:, 3 * D:]).then_inc(ld_w, 16)
            half = B * SK // 2
            sp.dma_start(ctxT_sb[:, 0:half], ctxT[:, 0:half]).then_inc(ld_ctx[0], 16)
            for piece in order:
                kind, b, u = piece
                if kind == "proj":
                    for k in range(1 + PARTS):
                        sp.wait_ge(parts_ready, 3 * b + min(k + 1, 3))
                        src = parts[:, b % 2, 0:PARTS, 0, :] if k == 0 else parts[:, b % 2, k - 1:k - 1 + PARTS, 1, :]
                        sp.dma_start(parts_dram[b, k].rearrange("p (i t) -> p i t", i=PARTS), src)\
                            .then_inc(stored[b][k], 16)
                    sp.wait_ge(zeroed, min(2 * b + 2, B + KBUF))
                    if b >= KBUF:
                        filled(sp, "s", ("exp", b - KBUF, NU - 1))
                    for x, k, c in [(qx, 0, c) for c in range(PARTS)] + [(kx, 1 + c, c) for c in range(PARTS)]:
                        sp.wait_ge(stored[b][k], 16)
                        sp.dma_start(x[c * PARTS * DK:(c + 1) * PARTS * DK, b % KBUF, :, :], parts_dram[b, k].rearrange(
                            "(h d) (i t) -> (d i) h t", d=DK, i=PARTS)).then_inc(spread[b], 16)
                    if b == 0:
                        sp.dma_start(tab_sb[:, :], tables).then_inc(ld_tab, 16)
                    if b == 2:
                        sp.dma_start(b1_sb[:, :], b1c).then_inc(ld_ffn, 16)
                        sp.wait_ge(blank_ready, 1)
                        sp.dma_start(sorted_dram[E * REGION:, :], blank[:, :]).then_inc(blanked, 16)
                if kind == "max" and 0 <= NU * (b - 1) + u < E:
                    e = NU * (b - 1) + u
                    filled(sp, "s", piece)
                    sp.dma_start(w2_sb[:, e, :, :].rearrange("p c d -> p (c d)"), w2T[:, e * FC * D:(e + 1) * FC * D])\
                        .then_inc(ld_ffn, 16)
                if kind == "rank" and b == B - 2:
                    sp.wait_ge(ends_ready, 1)
                    for e in range(E):
                        row = sp.value_load(end32[0:1, e:e + 1], min_val=0, max_val=(E - 1) * REGION + (B - 1) * S)
                        sp.dma_start(sorted_dram[bass.ds(row, LATE * P), :].rearrange("(n p) w -> p n w", p=P),
                                     blank[:, :].unsqueeze(1).to_broadcast([P, LATE, XW])).then_inc(blanked, 16)
                if kind == "shift":
                    taken(sp, "m", piece)
                    heads = slice(u * H // 2, (u + 1) * H // 2)
                    for i in range(2):
                        sp.dma_start(qx[MROW + i:MROW + i + 1, b % KBUF, heads, :].rearrange("o h (t q) -> o (h t) q", t=NT),
                                     mshift[:, b % 2, u, i, :]).then_inc(shifted[b][u], 16)
                    if b == 0 and u == 0:
                        sp.dma_start(x_sb[:, :, :], xtok.rearrange("(n p) d -> p n d", p=P)).then_inc(ld_x, 16)
                    if b == 0 and u == 1:
                        sp.dma_start(ctxT_sb[:, half:], ctxT[:, half:]).then_inc(ld_ctx[1], 16)
                        sp.dma_start(b2_sb[:, :, :].rearrange("p e d -> p (e d)"), b2r.partition_broadcast(P))\
                            .then_inc(ld_b2, 16)
            sp.wait_ge(table_ready, 1)
            experts, blocks = [], []

            def load_w1(i):
                if i == len(experts):
                    experts.extend(word_values(sp, eword32, i // EWORD, EBITS, EWORD, E - 1))
                if i >= WBUF:
                    filled(sp, "s", ("up", i - WBUF, 0))
                sp.dma_start(w1_t[i % WBUF].rearrange("p (a f) -> p a f", a=1),
                             w1T.rearrange("p (e f) -> p e f", e=E)[:, bass.ds(experts[i], 1), :])\
                             .then_inc(w1_full[i % WBUF], 16)

            def load_tokens(i):
                if i == len(blocks):
                    blocks.extend(word_values(sp, rword32, i // RWORD, RBITS, RWORD, E * REGION // P))
                if i == 0:
                    sp.wait_ge(placed, 16 * TILES)
                sp.dma_start(xt[i], sorted_dram[bass.ds(blocks[i] * P, P), :]).then_inc(xt_full[i], 16)

            for i in range(2):
                load_w1(i)
            sp.wait_ge(table_ready, 2)
            for i in range(FT_OFTEN):
                load_tokens(i)
                if i + 2 < FT_OFTEN:
                    load_w1(i + 2)
            with sp.If(tile_count(sp) > FT_OFTEN):
                for i in range(FT_OFTEN, FT):
                    load_w1(i)
                    load_tokens(i)

        @block.gpsimd
        def _(pool):
            pool.dma_start(rows_sb[:, :], rows.partition_broadcast(P)).then_inc(ld_rows, 16)
            signals = {}

            def own(ins, signal=pool_done):
                signals[signal.name] = signals.get(signal.name, 0) + 1
                ins.then_inc(signal, 1)
                pool.wait_ge(signal, signals[signal.name])

            own(pool.memset(ident[:, :], 0.0))
            own(pool.memset(maskb[:, :, :], 0.0))
            own(pool.affine_select(out=ident[:, :], in_=ident[:, :], compare_op=ALU.not_equal, fill=1.0, base=0,
                                   pattern=[[-1, P]], channel_multiplier=1))
            own(pool.affine_select(out=maskb[:, :, :], in_=maskb[:, :, :], compare_op=ALU.is_ge, fill=SHUT, base=0,
                                   pattern=[[0, 4], [-1, P]], channel_multiplier=1))
            own(pool.tensor_copy(identb[:, :], ident[:, :]), consts)
            for b in range(KBUF):
                own(pool.memset(qx[64:P, b, :, :].bitcast(U32), 0), zeroed)
                own(pool.memset(kx[64:P, b, :, :].bitcast(U32), 0))
                own(pool.memset(kx[MROW:MROW + 2, b, :, :].bitcast(U32), ONES2), zeroed)
            pool.wait_ge(ld_x, 16)
            pool.wait_ge(ld_rows, 16)
            own(pool.tensor_tensor(x_sb[:, :, :], x_sb[:, :, :],
                                   R(BO).unsqueeze(1).to_broadcast([P, TILES, D]), ALU.add), residual_ready)
            own(pool.memset(blank[:, :], 0.0))
            own(pool.memset(blank[:, D:D + 1].bitcast(I32), NOBODY), blank_ready)
            own(pool.memset(mhalf[:, :], -0.5))
            own(pool.memset(x2[:, :, D:XW], 0.0))
            own(pool.iota(x2[:, :, D].bitcast(I32), pattern=[[P, TILES]], base=0, channel_multiplier=1))
            own(pool.memset(onesb[:, :], 1.0))
            pool.wait_ge(ld_tab, 16)
            own(pool.tensor_copy(regionb[:, :], region[0:1, :]))
            own(pool.affine_select(out=before[:, :], in_=onesb[:, :], compare_op=ALU.is_gt, fill=0.0, base=0,
                                   pattern=[[1, P]], channel_multiplier=-1), consts)
            for kind, b, u in order:
                if kind == "exp" and u == NU - 1 and b + KBUF < B:
                    filled(pool, "s", (kind, b, u))
                    own(pool.memset(qx[MROW:MROW + 2, b % KBUF, :, :].bitcast(U32), 0), zeroed)
                if kind in ("out", "cross"):
                    pool.wait_ge(var_ready, norm_at[(kind, b, u)])
                    k = 0 if kind == "out" else 1
                    own(pool.tensor_tensor(rstd[:, k, :], var[:, k, :], mhalf[:, 0:NT], ALU.pow), rstd_ready)
                if kind == "rank":
                    if b == B - 1:
                        pool.wait_ge(blanked, 16 * (E + 1))
                    pool.wait_ge(ranked, b + 1)
                    for n in range(b * NT, (b + 1) * NT):
                        pool.indirect_dma_start(out=sorted_dram, out_offset=bass.IndirectOffsetOnAxis(ap=slot32[:, n:n + 1], axis=0),
                                                in_=x2[:, n, :], in_offset=None).then_inc(placed, 16)

            def reciprocal_deviation(i):
                pool.wait_ge(var_ready, norms + i + 1)
                own(pool.tensor_tensor(rstd[:, i % 2, 0:1], var[:, i % 2, 0:1], mhalf[:, 0:1], ALU.pow), rstd_ready)

            def write_tile(i):
                pool.wait_ge(yo_ready, i + 1)
                pool.indirect_dma_start(out=out, out_offset=bass.IndirectOffsetOnAxis(
                    ap=xt[i][:, D:D + 1].bitcast(I32), axis=0), in_=yo[i], in_offset=None,
                    bounds_check=B * S - 1, oob_is_err=False).then_inc(done, 16)

            def write_tiles(first, past):
                for i in range(first, past - 1):
                    reciprocal_deviation(i)
                    if i > first:
                        write_tile(i - 1)
                write_tile(past - 2)
                reciprocal_deviation(past - 1)
                write_tile(past - 1)
                pool.wait_ge(done, 16 * past)

            pool.wait_ge(table_ready, 1)
            count = tile_count(pool)
            write_tiles(*spans[0])
            with pool.If(count > FT_OFTEN):
                write_tiles(*spans[1])

        @block.scalar
        def _(act):
            act.wait_ge(ld_x0, 48)
            act.activation(bq_scaled[:, :], cols_sb[:, BQ:BQ + 1], ACT.Copy, scale=float(DK) ** -0.5)\
                .then_inc(bq_ready, 1)
            act.wait_ge(bq_ready, 1)
            for piece in order:
                kind, b, u = piece
                if kind == "proj":
                    qk, free = filled(act, "m", piece, 0)
                    if b >= 2:
                        act.wait_ge(parts_ready, 3 * (b - 1))
                    act.activation(qk32[:, b % 2, 0, :], qk[:, 0:S], ACT.Identity, bias=bq_scaled[:, :],
                                   scale=float(DK) ** -0.5)
                    act.activation(qk32[:, b % 2, 1, :], qk[:, S:2 * S], ACT.Identity,
                                   bias=cols_sb[:, BK:BK + 1]).then_inc(free, 1)
                    taken(act, "m", piece, 0)
                    if b >= 2:
                        for k in range(1 + PARTS):
                            act.wait_ge(stored[b - 2][k], 16)
                    act.activation(parts[:, b % 2, 0, :, :], qk32[:, b % 2, :, :], ACT.Copy).then_inc(first_part, 1)
                    vp, free = filled(act, "m", piece, 1)
                    act.wait_ge(vx_ready, 1)
                    if b >= KBUF:
                        act.wait_ge(pv_done, 4 * (b - KBUF + 1))
                    act.activation(vx[:, b % KBUF, :, :, 0:DK].rearrange("p t h d -> p (t h) d"),
                                   vp[:, 0:NT * D].rearrange("p (t h d) -> p (t h) d", t=NT, h=H), ACT.Copy)\
                                   .then_inc(free, 1)
                if kind == "ctx":
                    k2, free = filled(act, "m", piece, 0)
                    if b >= KBUF:
                        filled(act, "s", ("relu", b - KBUF, 0))
                    act.activation(k2T[:, b % KBUF, :], k2[:, :], ACT.Identity, bias=cols_sb[:, XBK:XBK + 1])\
                        .then_inc(free, 1)
                if kind == "shift":
                    mt, _f = filled(act, "m", piece)
                    if b >= 2:
                        act.wait_ge(shifted[b - 2][u], 32)
                    act.activation(mshift[:, b % 2, u, 0, :], mt[0:H, 0:P], ACT.Copy, scale=-1.0).then_inc(mhi_ready, 1)
                if kind == "exp":
                    sc, free = filled(act, "s", piece)
                    k = NU * b + u
                    if k >= EBUF:
                        ob, ou = divmod(k - EBUF, NU)
                        act.wait_ge(pv_done, 4 * ob + (2 if ou < 3 else 4))
                    act.activation(es[:, k % EBUF, :], sc[:, :], ACT.Exp).then_inc(free, 1)
                if kind == "evac":
                    act.wait_ge(pv_done, 4 * b + 4)
                    if b:
                        act.wait_ge(turned, b)
                    act.activation(osb[:, 0:2, :], ps_o[:, 0:512].rearrange("p (g q) -> p g q", g=2), ACT.Copy)
                    act.activation(osb[:, 2:4, :], ps_o[:, 512:1024].rearrange("p (g q) -> p g q", g=2),
                                   ACT.Copy).then_inc(osb_ready, 1)
                if kind == "back":
                    at, free = filled(act, "m", piece)
                    act.activation(attnT[:, :], at[:, 0:S], ACT.Identity, bias=cols_sb[:, BV:BV + 1]).then_inc(free, 1)
                if kind == "x1t":
                    at, free = filled(act, "m", piece)
                    act.activation(x1T[:, :], at[:, 0:S], ACT.Copy).then_inc(free, 1)
                if kind == "q2":
                    at, free = filled(act, "m", piece)
                    act.activation(q2T[:, :], at[:, 0:S], ACT.Identity, bias=cols_sb[:, XBQ:XBQ + 1]).then_inc(free, 1)
                if kind == "relu":
                    at, free = filled(act, "s", piece)
                    act.activation(sc2[:, :, :], at[:, :].rearrange("p (k q) -> p k q", k=KT), ACT.Relu)\
                        .then_inc(free, 1)
                if kind == "x2t":
                    at, free = filled(act, "m", piece)
                    act.activation(x2T[:, :], at[:, 0:S], ACT.Copy).then_inc(free, 1)
            act.wait_ge(ld_ffn, 16 * (E + 1))
            act.wait_ge(table_ready, 1)
            experts = tile_experts(act)
            count = tile_count(act)

            def tiles(first, past):
                for piece in expert_schedule(first, past):
                    kind, i, _u = piece
                    if kind == "gather":
                        at, free = filled(act, "m", piece)
                        if i >= 2:
                            filled(act, "s", ("up", i - 2, 0))
                        act.activation(xsT[i % 2], at[:, 0:P], ACT.Copy).then_inc(free, 1)
                    if kind == "up":
                        at, free = filled(act, "s", piece)
                        if i >= 2:
                            filled(act, "m", ("down", i - 2, 0))
                        for c in range(FC):
                            ins = act.activation(hT[i % 2][:, c * P:(c + 1) * P], at[:, c * P:(c + 1) * P], ACT.Relu,
                                                 bias=b1_sb[:, bass.ds(experts[i] * FC + c, 1)])
                        ins.then_inc(free, 1)

            tiles(*spans[0])
            with act.If(count > FT_OFTEN):
                tiles(*spans[1])

        @block.tensor
        def _(pe):
            pe.wait_ge(ld_x0, 48)

            def keep_warm(times):
                for _i in range(times):
                    pe.matmul(ps_o[:, 0:512], identb[:, :], maskb[:, :, :], start=True, stop=True)

            for piece in order:
                kind, b, u = piece
                if kind == "proj":
                    if b:
                        pe.wait_ge(ld_xT, 16)
                    xTb = xT_sb[:, b * S:(b + 1) * S]
                    qk, full = vacant(pe, "m", piece, 0)
                    pe.matmul(qk[:, 0:S], W(WQ), xTb, start=True, stop=True)
                    pe.matmul(qk[:, S:2 * S], W(WK), xTb, start=True, stop=True).then_inc(full, 1)
                    v, full = vacant(pe, "m", piece, 1)
                    for t in range(NT):
                        mm = pe.matmul(v[:, t * D:(t + 1) * D], xTb[:, t * P:(t + 1) * P], W(WV), start=True, stop=True)
                    mm.then_inc(full, 1)
                if kind == "ctx":
                    pe.wait_ge(ld_ctx[2 * b // B], 16)
                    pe.wait_ge(ld_w, 16)
                    cT = ctxT_sb[:, b * SK:(b + 1) * SK]
                    k2, full = vacant(pe, "m", piece, 0)
                    pe.matmul(k2[:, :], W(XK), cT, start=True, stop=True).then_inc(full, 1)
                    v, full = vacant(pe, "m", piece, 1)
                    for t in range(KT):
                        mm = pe.matmul(v[:, t * D:(t + 1) * D], cT[:, t * P:(t + 1) * P], W(XV), start=True, stop=True)
                    mm.then_inc(full, 1)
                if kind == "max":
                    if u == 0:
                        pe.wait_ge(spread[b], 16 * 2 * PARTS)
                        pe.wait_ge(zeroed, min(2 * b + 2, B + KBUF))
                        if b == 0:
                            pe.wait_ge(consts, 1)
                    sc, full = vacant(pe, "s", piece)
                    t, h0, _n = max_unit(u)
                    keys = (t + 1) * P
                    hs = 512 // keys
                    for bank in range(2):
                        o = sc[:, bank * 512:(bank + 1) * 512].rearrange("p (h k) -> p h k", h=hs)
                        pe.matmul(o[:, :, t * P:keys], identb[:, :], maskb[:, 0:hs, :], start=True, stop=False,
                                  skip_group_check=True)
                        for j in range(hs):
                            h = h0 + bank * hs + j
                            mm = pe.matmul(o[:, j, :], qx[:, b % KBUF, h, t * P:(t + 1) * P], kx[:, b % KBUF, h, 0:keys],
                                           start=False, stop=(j == hs - 1), skip_group_check=True)
                    mm.then_inc(full, 1)
                if kind == "warm":
                    pe.wait_ge(attn_ready, B)
                    keep_warm(u)
                if kind == "shift":
                    for last in (NU // 2 * (u + 1) - 2, NU // 2 * (u + 1) - 1):
                        taken(pe, "s", ("max", b, last))
                    mt, full = vacant(pe, "m", piece)
                    pe.transpose(mt[0:H, 0:P], mx[:, b % 2, u * H // 2:(u + 1) * H // 2, :].rearrange("p h t -> p (h t)"),
                                 ident[:, :]).then_inc(full, 1)
                if kind == "exp":
                    if u % (NU // 2) == 0:
                        pe.wait_ge(shifted[b][u // (NU // 2)], 32)
                    sc, full = vacant(pe, "s", piece)
                    kt, h0, n = UNITS[u]
                    qs = S - kt * P
                    for j in range(n):
                        h = h0 + j
                        mm = pe.matmul(sc[:, j * qs:(j + 1) * qs], kx[:, b % KBUF, h, kt * P:(kt + 1) * P],
                                       qx[:, b % KBUF, h, kt * P:S], start=True, stop=True)
                    mm.then_inc(full, 1)
                if kind == "pv":
                    pe.wait_ge(p_ready, NU * b + (3 if u < 2 else 6))
                    if u == 0:
                        taken(pe, "m", ("proj", b, 0), 1)
                        if b:
                            pe.wait_ge(attn_ready, b)
                    for kt in range(NT):
                        for j in range(4):
                            h = 4 * u + j
                            k, at = where(kt, h)
                            qs = S - kt * P
                            mm = pe.matmul(ps_o[VW * j:VW * (j + 1), u * S + kt * P:(u + 1) * S], vx[:, b % KBUF, kt, h, :],
                                           es[:, (NU * b + k) % EBUF, at:at + qs], start=(kt == 0), stop=(kt == 1))
                    mm.then_inc(pv_done, 1)
                if kind == "turn":
                    pe.wait_ge(osb_ready, b + 1)
                    for t in range(NT):
                        for g in range(4):
                            mm = pe.transpose(ps_o[:, t * 512 + g * P:t * 512 + (g + 1) * P],
                                              osb[:, g, t * P:(t + 1) * P], ident[:, :])
                    mm.then_inc(turned, 1)
                if kind == "back":
                    pe.wait_ge(attn_ready, b + 1)
                    at, full = vacant(pe, "m", piece)
                    for t in range(NT):
                        mm = pe.transpose(at[:, t * P:(t + 1) * P], attn[:, t, :], ident[:, :])
                    mm.then_inc(full, 1)
                if kind == "out":
                    taken(pe, "m", ("back", b, 0))
                    y, full = vacant(pe, "m", piece)
                    for t in range(NT):
                        mm = pe.matmul(y[:, t * D:(t + 1) * D], attnT[:, t * P:(t + 1) * P], W(WO), start=True, stop=True)
                    mm.then_inc(full, 1)
                if kind == "x1t":
                    pe.wait_ge(x1_ready, b + 1)
                    at, full = vacant(pe, "m", piece)
                    for t in range(NT):
                        mm = pe.transpose(at[:, t * P:(t + 1) * P], x1[:, b * NT + t, :], ident[:, :])
                    mm.then_inc(full, 1)
                if kind == "q2":
                    taken(pe, "m", ("x1t", b, 0))
                    at, full = vacant(pe, "m", piece)
                    pe.matmul(at[:, 0:S], W(XQ), x1T[:, :], start=True, stop=True).then_inc(full, 1)
                if kind == "relu":
                    taken(pe, "m", ("q2", b, 0))
                    taken(pe, "m", ("ctx", b, 0))
                    at, full = vacant(pe, "s", piece)
                    for k in range(KT):
                        mm = pe.matmul(at[:, k * S:(k + 1) * S], k2T[:, b % KBUF, k * P:(k + 1) * P], q2T[:, :],
                                       start=True, stop=True)
                    mm.then_inc(full, 1)
                if kind == "cross":
                    taken(pe, "s", ("relu", b, 0))
                    taken(pe, "m", ("ctx", b, 0), 1)
                    at, full = vacant(pe, "m", piece)
                    for t in range(NT):
                        for k in range(KT):
                            mm = pe.matmul(at[:, t * D:(t + 1) * D], sc2[:, k, t * P:(t + 1) * P], v2[:, b % KBUF, k, :],
                                           start=(k == 0), stop=(k == KT - 1))
                    mm.then_inc(full, 1)
                if kind == "x2t":
                    pe.wait_ge(x2_ready, b + 1)
                    at, full = vacant(pe, "m", piece)
                    for t in range(NT):
                        mm = pe.transpose(at[:, t * P:(t + 1) * P], x2[:, b * NT + t, 0:D], ident[:, :])
                    mm.then_inc(full, 1)
                if kind == "route":
                    taken(pe, "m", ("x2t", b, 0))
                    at, full = vacant(pe, "m", piece)
                    for t in range(NT):
                        mm = pe.matmul(at[:, t * E:(t + 1) * E], x2T[:, t * P:(t + 1) * P], W(WR),
                                       start=True, stop=True)
                    mm.then_inc(full, 1)
                if kind == "rank":
                    pe.wait_ge(hot_ready, b + 1)
                    if b == 0:
                        pe.wait_ge(consts, 2)
                    at, full = vacant(pe, "m", piece)
                    for t in range(NT + 1):
                        n = b * NT + t
                        o = at[:, t * E:(t + 1) * E]
                        if t < NT:
                            pe.matmul(o, onesb[0:1, :], regionb[0:1, :], start=True, stop=False)
                            pe.matmul(o, before[:, :], hotb[:, n, :], start=False, stop=(n == 0))
                        for m in range(n):
                            mm = pe.matmul(o, onesb[:, :], hotb[:, m, :], start=(m == 0 and t == NT), stop=(m == n - 1))
                    mm.then_inc(full, 1)
            pe.wait_ge(ld_ffn, 16 * (E + 1))
            pe.wait_ge(table_ready, 1)
            experts = tile_experts(pe)
            count = tile_count(pe)
            keep_warm(12)

            def tiles(first, past):
                for piece in expert_schedule(first, past):
                    kind, i, _u = piece
                    if kind == "gather":
                        pe.wait_ge(xt_full[i], 16)
                        at, full = vacant(pe, "m", piece)
                        pe.transpose(at[:, 0:P], xt[i][:, 0:D], ident[:, :]).then_inc(full, 1)
                    if kind == "up":
                        pe.wait_ge(w1_full[i % WBUF], 16 * (i // WBUF + 1))
                        taken(pe, "m", ("gather", i, 0))
                        at, full = vacant(pe, "s", piece)
                        for c in range(FC):
                            mm = pe.matmul(at[:, c * P:(c + 1) * P], w1_t[i % WBUF][:, c * P:(c + 1) * P], xsT[i % 2],
                                           start=True, stop=True)
                        mm.then_inc(full, 1)
                    if kind == "down":
                        taken(pe, "s", ("up", i, 0))
                        at, full = vacant(pe, "m", piece)
                        w2 = w2_sb[:, bass.ds(experts[i], 1), :, :].rearrange("p a c d -> p (a c) d")
                        for c in range(FC):
                            mm = pe.matmul(at[:, 0:D], hT[i % 2][:, c * P:(c + 1) * P], w2[:, c, :],
                                           start=(c == 0), stop=(c == FC - 1))
                        mm.then_inc(full, 1)

            tiles(*spans[0])
            with pe.If(count > FT_OFTEN):
                tiles(*spans[1])

        @block.vector
        def _(v):
            link = [0]

            def mark(ins):
                link[0] += 1
                ins.then_inc(dve, 1)
                return link[0]

            def own(ins):
                v.wait_ge(dve, mark(ins))

            def variance(k):
                for t in range(NT):
                    ins = v.bn_stats(stats[:, t, :], z[k][:, t, :])
                own(ins)
                for t in range(NT):
                    ins = v.bn_aggr(mv[:, k, t, :], stats[:, t, :])
                own(ins)
                v.tensor_scalar(var[:, k, :], mv[:, k, :, 1], EPS, None, ALU.add).then_inc(var_ready, 1)

            def normalise(k, dst, ready):
                for t in range(NT):
                    ins = v.tensor_scalar(dst[:, t, :], z[k][:, t, :], mv[:, k, t, 0:1], rstd[:, k, t:t + 1],
                                          ALU.subtract, ALU.mult)
                ins.then_inc(ready, 1)

            v.memset(vx[:, :, :, :, :].rearrange("p b t h w -> p (b t h) w")[:, :, DK + 1:VW], 0.0)
            v.memset(vx[:, :, :, :, :].rearrange("p b t h w -> p (b t h) w")[:, :, DK:DK + 1], 1.0)\
                .then_inc(vx_ready, 1)
            for piece in order:
                kind, b, u = piece
                if kind == "proj":
                    v.wait_ge(first_part, b + 1)
                    qk, r = qk32[:, b % 2, :, :], rest[:, b % 2, :, :]
                    p = [parts[:, b % 2, i, :, :] for i in range(PARTS)]
                    rests = [mark(v.tensor_tensor(r[:, w, :], qk[:, w, :], p[0][:, w, :], ALU.subtract)) for w in range(2)]
                    seconds = []
                    for w in range(2):
                        v.wait_ge(dve, rests[w])
                        seconds.append(mark(v.tensor_copy(p[1][:, w, :], r[:, w, :])))
                    for w in range(2):
                        v.wait_ge(dve, seconds[w])
                        v.tensor_tensor(p[2][:, w, :], r[:, w, :], p[1][:, w, :], ALU.subtract).then_inc(parts_ready, 1)
                    v.tensor_copy(parts[:, b % 2, PARTS:2 * PARTS - 1, 1, :], parts[:, b % 2, 0:PARTS - 1, 1, :])\
                        .then_inc(parts_ready, 1)
                if kind == "ctx":
                    vp, free = filled(v, "m", piece, 1)
                    v.wait_ge(ld_rows, 16)
                    if b >= KBUF:
                        filled(v, "m", ("cross", b - KBUF, 0))
                    v.tensor_tensor(v2[:, b % KBUF, :, :], vp[:, :].rearrange("p (k d) -> p k d", k=KT),
                                    R(XBV).unsqueeze(1).to_broadcast([P, KT, D]), ALU.add).then_inc(free, 1)
                if kind == "max":
                    sc, free = filled(v, "s", piece)
                    t, h0, n = max_unit(u)
                    if u == 0 and b >= 2:
                        filled(v, "m", ("shift", b - 2, 1))
                    v.tensor_reduce(mx[:, b % 2, h0:h0 + n, t], sc[:, :].rearrange("p (h k) -> p h k", h=n), AX.X,
                                    ALU.max).then_inc(free, 1)
                if kind == "shift":
                    mt, free = filled(v, "m", piece)
                    v.wait_ge(mhi_ready, 2 * b + u + 1)
                    v.scalar_tensor_tensor(out=mshift[:, b % 2, u, 1, :], in0=mt[0:H, 0:P], scalar=-1.0,
                                           in1=mshift[:, b % 2, u, 0, :], op0=ALU.mult, op1=ALU.subtract)\
                                           .then_inc(free, 1)
                if kind == "exp":
                    v.wait_ge(ld_tab, 16)
                    taken(v, "s", piece)
                    kt, h0, nh = UNITS[u]
                    qs = S - kt * P
                    e = es[:, (NU * b + u) % EBUF, :].rearrange("p (h q) -> p h q", h=nh)
                    v.scalar_tensor_tensor(out=e, in0=e, scalar=CEIL, in1=decay[:, 0:qs].unsqueeze(1).to_broadcast([P, nh, qs]),
                                           op0=ALU.min, op1=ALU.mult).then_inc(p_ready, 1)
                if kind == "turn":
                    v.wait_ge(turned, b + 1)
                    o = ps_o[:, :].rearrange("p (t h w) -> p t h w", t=NT, h=H)
                    if b:
                        filled(v, "m", ("back", b - 1, 0))
                    for t in range(NT):
                        ins = v.reciprocal(rden[:, t, :], o[:, t, :, DK])
                    own(ins)
                    for t in range(NT):
                        ins = v.tensor_tensor(attn[:, t, :].rearrange("p (h d) -> p h d", h=H), o[:, t, :, 0:DK],
                                              rden[:, t, :].unsqueeze(2).to_broadcast([P, H, DK]), ALU.mult)
                        if t == 0:
                            own(ins)
                    ins.then_inc(attn_ready, 1)
                if kind == "out":
                    y, free = filled(v, "m", piece)
                    v.wait_ge(residual_ready, 1)
                    if b:
                        v.wait_ge(x1_ready, b)
                    ins = v.tensor_tensor(z[0][:, :, :], y[:, 0:NT * D].rearrange("p (t d) -> p t d", t=NT),
                                          x_sb[:, b * NT:(b + 1) * NT, :], ALU.add)
                    ins.then_inc(free, 1)
                    taken(v, "m", piece)
                    variance(0)
                if kind == "norm1":
                    v.wait_ge(rstd_ready, norm_at[("out", b, 0)])
                    normalise(0, x1[:, b * NT:(b + 1) * NT, :], x1_ready)
                if kind == "cross":
                    y, free = filled(v, "m", piece)
                    v.wait_ge(x1_ready, b + 1)
                    if b:
                        v.wait_ge(x2_ready, b)
                    ins = v.tensor_tensor(z[1][:, :, :], y[:, 0:NT * D].rearrange("p (t d) -> p t d", t=NT),
                                          x1[:, b * NT:(b + 1) * NT, :], ALU.add)
                    ins.then_inc(free, 1)
                    taken(v, "m", piece)
                    variance(1)
                if kind == "norm2":
                    v.wait_ge(rstd_ready, norm_at[("cross", b, 0)])
                    normalise(1, x2[:, b * NT:(b + 1) * NT, 0:D], x2_ready)
                if kind == "route":
                    at, free = filled(v, "m", piece)
                    if b:
                        v.wait_ge(hot_ready, b)
                    v.tensor_tensor(lg[:, :, :], at[:, 0:NT * E].rearrange("p (t e) -> p t e", t=NT),
                                    R(BR).unsqueeze(1).to_broadcast([P, NT, E]), ALU.add).then_inc(free, 1)
                    taken(v, "m", piece)
                    own(v.tensor_reduce(lgmax[:, :], lg[:, :, :], AX.X, ALU.max))
                    for t in range(NT):
                        ins = v.scalar_tensor_tensor(out=hot[:, t, :], in0=lg[:, t, :], scalar=lgmax[:, t:t + 1], in1=rank8,
                                                     op0=ALU.is_ge, op1=ALU.mult)
                    own(ins)
                    own(v.tensor_reduce(lgmax[:, :], hot[:, :, :], AX.X, ALU.max))
                    v.tensor_tensor(hotb[:, b * NT:(b + 1) * NT, :], hot[:, :, :],
                                    lgmax[:, :].unsqueeze(2).to_broadcast([P, NT, E]), ALU.is_equal)\
                                    .then_inc(hot_ready, 1)
                if kind == "rank":
                    at, free = filled(v, "m", piece)
                    own(v.tensor_tensor(lg[:, :, :], at[:, 0:NT * E].rearrange("p (t e) -> p t e", t=NT),
                                        hotb[:, b * NT:(b + 1) * NT, :], ALU.mult))
                    own(v.tensor_reduce(slotf[:, :], lg[:, :, :], AX.X, ALU.add))
                    v.tensor_copy(slot32[:, b * NT:(b + 1) * NT], slotf[:, :]).then_inc(ranked, 1)
                    if b == B - 2:
                        v.tensor_tensor(end32[:, :], at[0:1, NT * E:(NT + 1) * E], region[0:1, :], ALU.add)\
                            .then_inc(ends_ready, 1)
                    v.tensor_copy(total[:, :], at[0:1, NT * E:(NT + 1) * E]).then_inc(free, 1)
            taken(v, "m", ("rank", B - 1, 0))
            own(v.tensor_tensor(more[:, :, :], total[:, :].unsqueeze(2).to_broadcast([1, E, E]),
                                fills.unsqueeze(1).to_broadcast([1, E, E]), ALU.is_gt))
            own(v.tensor_reduce(ntile[:, :], more[:, :, :], AX.X, ALU.add))
            own(v.tensor_tensor(more[:, :, :], lower, ntile[:, :].unsqueeze(1).to_broadcast([1, E, E]), ALU.mult))
            own(v.tensor_reduce(ends[:, :], more[:, :, :], AX.X, ALU.add))
            own(v.tensor_tensor(past[:, :, :], ends[:, :].unsqueeze(1).to_broadcast([1, FTP, E]), number, ALU.is_le))
            own(v.tensor_reduce(texp[:, :], past[:, :, :], AX.X, ALU.add))
            own(v.tensor_tensor(past2[:, :, :], past[:, :, :], ntile[:, :].unsqueeze(1).to_broadcast([1, FTP, E]), ALU.mult))
            own(v.tensor_reduce(tfirst[:, :], past2[:, :, :], AX.X, ALU.add))
            own(v.scalar_tensor_tensor(out=past[:, :, 0], in0=texp[:, :], scalar=E - 1.0, in1=eplace,
                                       op0=ALU.min, op1=ALU.mult))
            own(v.tensor_reduce(eword[:, :], past[:, 0:FTE, 0].rearrange("p (k i) -> p k i", i=EWORD), AX.X, ALU.add))
            v.tensor_copy(ntiles32[:, :], ends[:, E - 1:E])
            v.tensor_copy(eword32[:, :], eword[:, :]).then_inc(table_ready, 1)
            own(v.scalar_tensor_tensor(out=tfirst[:, :], in0=texp[:, :], scalar=float(REGION // P), in1=tfirst[:, :],
                                       op0=ALU.mult, op1=ALU.subtract))
            own(v.tensor_tensor(tfirst[:, :], tfirst[:, :], number[:, :, 0], ALU.add))
            own(v.scalar_tensor_tensor(out=tfirst[:, :], in0=tfirst[:, :], scalar=float(E * REGION // P), in1=rplace,
                                       op0=ALU.min, op1=ALU.mult))
            own(v.tensor_reduce(rword[:, :], tfirst[:, 0:FTR].rearrange("p (k i) -> p k i", i=RWORD), AX.X, ALU.add))
            v.tensor_copy(rword32[:, :], rword[:, :]).then_inc(table_ready, 1)
            v.wait_ge(table_ready, 2)
            v.wait_ge(ld_b2, 16)
            experts = tile_experts(v)

            def residual(i):
                v.wait_ge(xt_full[i], 16)
                return v.tensor_tensor(xres[i % 2], xt[i][:, 0:D],
                                       b2_sb[:, bass.ds(experts[i], 1), :].rearrange("p a d -> p (a d)"), ALU.add)

            def normalise_tile(i):
                k = i % 2
                v.wait_ge(rstd_ready, norms + i + 1)
                v.tensor_scalar(yo[i], zt[k], mv[:, k, 0, 0:1], rstd[:, k, 0:1], ALU.subtract, ALU.mult)\
                    .then_inc(yo_ready, 1)

            def tiles(first, past):
                own(residual(first))
                for piece in expert_schedule(first, past):
                    kind, i, _u = piece
                    if kind == "down":
                        at, free = filled(v, "m", piece)
                        k = i % 2
                        if i == past - 1:
                            normalise_tile(i - 1)
                        v.tensor_tensor(zt[k], at[:, 0:D], xres[k], ALU.add).then_inc(free, 1)
                        taken(v, "m", piece)
                        own(v.bn_stats(st[k], zt[k]))
                        own(v.bn_aggr(mv[:, k, 0, :], st[k]))
                        v.tensor_scalar(var[:, k, 0:1], mv[:, k, 0, 1:2], EPS, None, ALU.add).then_inc(var_ready, 1)
                        if first < i < past - 1:
                            normalise_tile(i - 1)
                        if i + 1 < past:
                            own(residual(i + 1))
                normalise_tile(past - 1)

            count = tile_count(v)
            tiles(*spans[0])
            with v.If(count > FT_OFTEN):
                tiles(*spans[1])


NTAB = S + 3 * E + E * E + FTP * E + 2 * FTP


def shape_tables(np):
    late = np.arange(S)[None, :] - np.arange(P)[:, None]
    decay = np.where(late >= 0, np.maximum(late, 1).astype(np.float64) ** -DECAY, 0.0)
    e = np.arange(E)
    flat = [E - e, REGION * e, P * e, (e[None, :] <= e[:, None]).ravel(), np.repeat(np.arange(FTP), E),
            1 << EBITS * (np.arange(FTP) % EWORD), 1 << RBITS * (np.arange(FTP) % RWORD)]
    flat = np.concatenate(flat)
    return np.concatenate([decay, np.broadcast_to(flat, (P, flat.size))], axis=1).astype(np.float32)


def max_unit(u):
    half, k = divmod(u, NU // 2)
    return (0, 8 * half, 8) if k == 0 else (1, 8 * half + 4 * (k - 1), 4)


def where(kt, h):
    for k, (t, h0, n) in enumerate(UNITS):
        if t == kt and h0 <= h < h0 + n:
            return k, (h - h0) * (S - kt * P)


def kernel(**inputs):
    import numpy as np
    import concourse.bacc as bacc
    from concourse.bass_utils import run_bass_kernel_spmd as run

    a = {k: np.asarray(v) for k, v in inputs.items()}
    arrays = {
        "xtok": a["x"].reshape(B * S, D),
        "xT": a["x"].reshape(B * S, D).T,
        "ctxT": a["ctx_1024"].reshape(B * SK, D).T,
        "wts": np.concatenate([a["L0_attn_Wq"], a["L0_attn_Wk"], a["L0_attn_Wv"], a["L0_attn_Wo"], a["L0_xattn_Wq"].T,
                               a["L0_xattn_Wk"].T, a["L0_xattn_Wv"].T, a["L0_ffn_Wr"].T], axis=1),
        "cols": np.stack([a["L0_attn_bq"], a["L0_attn_bk"], a["L0_xattn_bq"], a["L0_xattn_bk"], a["L0_attn_bv"]], axis=1),
        "rows": np.concatenate([a["L0_attn_bo"], a["L0_xattn_bv"], a["L0_ffn_br"]]),
        "w1T": a["L0_ffn_W1"].transpose(2, 0, 1).reshape(D, E * FF),
        "w2T": a["L0_ffn_W2"].reshape(E, D, FC, P).transpose(3, 0, 2, 1).reshape(P, E * FC * D),
        "b1c": a["L0_ffn_b1"].reshape(E, FC, P).transpose(2, 0, 1).reshape(P, E * FC),
        "b2r": a["L0_ffn_b2"].reshape(E * D),
        "tables": shape_tables(np),
    }
    nc = bacc.Bacc("TRN2", target_bir_lowering=False, num_devices=1)
    args = []
    for name, v in arrays.items():
        arrays[name] = np.ascontiguousarray(v)
        args.append(nc.dram_tensor(name, v.shape, mybir.dt.from_np(v.dtype), kind="ExternalInput").ap())
    args.append(nc.dram_tensor("out", (B * S, D), F32, kind="ExternalOutput").ap())
    decoder_kernel(nc, *args)
    r = run(nc, [arrays], core_ids=[0])
    return r.results[0]["out"].reshape(B, S, D)
```
